# Optimizing a Trainium2 kernel written in Bass

```python
import numpy as np
import jax
import jax.numpy as jnp

def _softmax(x, axis=-1):
    return jax.nn.softmax(x, axis=axis)

def _gelu(x):
    return jax.nn.gelu(x, approximate=True)

def _silu(x):
    return jax.nn.silu(x)

def _sigmoid(x):
    return jax.nn.sigmoid(x)

def _layernorm(x, axis=-1, eps=1e-05):
    m = jnp.mean(x, axis=axis, keepdims=True)
    v = jnp.var(x, axis=axis, keepdims=True)
    return (x - m) / jnp.sqrt(v + eps)

def _scatter_add(tgt, idx, src, axis=0):
    return tgt.at[idx].add(src)

def _segment_sum(src, seg, n):
    return jax.ops.segment_sum(src, seg, n)
kernel_name = 'mk_lm_tower_d1_tok_ids4096_r4_9bf0c8'

def setup_inputs(seed: int=0):
    np.random.seed(seed)
    _w = jnp.asarray

    def _rec_inputs():
        import jax
        import jax.numpy as jnp
        _rk = jax.random.key(seed)
        x = jax.random.randint(jax.random.fold_in(_rk, 1), (4, 512), 0, 12564, jnp.int32)
        return x
    x = _rec_inputs()

    def _L0_tok_setup():
        import jax, jax.numpy as jnp
        import numpy as np
        VOCAB = 50257
        EMBED_DIM = 1024
        R = 16
        ALPHA = 32
        SCALING = ALPHA / R
        key = jax.random.key(seed)
        k_x, k_a, k_b = jax.random.split(key, 3)
        x = jax.random.randint(k_x, (4, 1024), 0, VOCAB, dtype=jnp.int64 if jax.config.jax_enable_x64 else jnp.int32)
        A = jax.random.normal(k_a, (R, VOCAB), dtype=jnp.float32)
        B = jax.random.normal(k_b, (EMBED_DIM, R), dtype=jnp.float32)
        return {'x': x, 'A': A, 'B': B}
    _L0_tok_all = _L0_tok_setup()
    _L0_tok_in = {k: v for k, v in _L0_tok_all.items() if k in ('A', 'B')}
    del _L0_tok_all

    def _L0_attn_setup():
        import jax, jax.numpy as jnp
        import numpy as np
        B, N, D = (8, 256, 1024)
        H = 8
        HEAD_DIM = D // H
        E = HEAD_DIM // H
        key = jax.random.key(seed)
        ks = jax.random.split(key, 7)
        s = 0.02
        return {'x': jax.random.normal(ks[0], (B, N, D), dtype=jnp.float32), 'Wqk_w': jax.random.normal(ks[1], (2 * HEAD_DIM, D), dtype=jnp.float32) * s, 'Wqk_b': jnp.zeros((2 * HEAD_DIM,), dtype=jnp.float32), 'Wv_w': jax.random.normal(ks[2], (HEAD_DIM, D), dtype=jnp.float32) * s, 'Wv_b': jnp.zeros((HEAD_DIM,), dtype=jnp.float32), 'Wo_w': jax.random.normal(ks[3], (D, HEAD_DIM), dtype=jnp.float32) * s, 'Wo_b': jnp.zeros((D,), dtype=jnp.float32)}
    _L0_attn_all = _L0_attn_setup()
    _L0_attn_in = {k: v for k, v in _L0_attn_all.items() if k in ('Wqk_w', 'Wqk_b', 'Wv_w', 'Wv_b', 'Wo_w', 'Wo_b')}
    del _L0_attn_all

    def _L0_ffn_setup():
        import jax, jax.numpy as jnp
        import numpy as np
        H = 1024
        I = 3584
        G = 128

        def dequant(q, s, g=G):
            O, In = q.shape
            return (q.reshape(O, In // g, g).astype(s.dtype) * s[:, :, None]).reshape(O, In)
        key = jax.random.key(seed)
        ks = jax.random.split(key, 7)
        x = jax.random.normal(ks[0], (2, 512, H), dtype=jnp.float32)

        def mk_qlinear(kq, ksc, out_d, in_d):
            q = jax.random.randint(kq, (out_d, in_d), -8, 8, dtype=jnp.int32)
            s = jax.random.uniform(ksc, (out_d, in_d // G), dtype=jnp.float32, minval=0.005, maxval=0.02)
            return (q, s)
        gate_q, gate_s = mk_qlinear(ks[1], ks[2], I, H)
        up_q, up_s = mk_qlinear(ks[3], ks[4], I, H)
        down_q, down_s = mk_qlinear(ks[5], ks[6], H, I)
        return {'x': x, 'gate_q': gate_q, 'gate_s': gate_s, 'up_q': up_q, 'up_s': up_s, 'down_q': down_q, 'down_s': down_s}
    _L0_ffn_all = _L0_ffn_setup()
    _L0_ffn_in = {k: v for k, v in _L0_ffn_all.items() if k in ('gate_q', 'gate_s', 'up_q', 'up_s', 'down_q', 'down_s')}
    del _L0_ffn_all
    return {'x': x, 'L0_tok_A': _L0_tok_in['A'], 'L0_tok_B': _L0_tok_in['B'], 'L0_attn_Wqk_w': _L0_attn_in['Wqk_w'], 'L0_attn_Wqk_b': _L0_attn_in['Wqk_b'], 'L0_attn_Wv_w': _L0_attn_in['Wv_w'], 'L0_attn_Wv_b': _L0_attn_in['Wv_b'], 'L0_attn_Wo_w': _L0_attn_in['Wo_w'], 'L0_attn_Wo_b': _L0_attn_in['Wo_b'], 'L0_ffn_gate_q': _L0_ffn_in['gate_q'], 'L0_ffn_gate_s': _L0_ffn_in['gate_s'], 'L0_ffn_up_q': _L0_ffn_in['up_q'], 'L0_ffn_up_s': _L0_ffn_in['up_s'], 'L0_ffn_down_q': _L0_ffn_in['down_q'], 'L0_ffn_down_s': _L0_ffn_in['down_s']}

def reference(x, L0_tok_A, L0_tok_B, L0_attn_Wqk_w, L0_attn_Wqk_b, L0_attn_Wv_w, L0_attn_Wv_b, L0_attn_Wo_w, L0_attn_Wo_b, L0_ffn_gate_q, L0_ffn_gate_s, L0_ffn_up_q, L0_ffn_up_s, L0_ffn_down_q, L0_ffn_down_s):
    import jax
    import jax.numpy as jnp

    def _L0_tok_ref(x, A, B):
        import jax, jax.numpy as jnp
        import numpy as np
        VOCAB = 50257
        EMBED_DIM = 1024
        R = 16
        ALPHA = 32
        SCALING = ALPHA / R
        low = A.T[x]
        return jnp.einsum('bsr,dr->bsd', low, B) * SCALING

    def _L0_attn_ref(x, Wqk_w, Wqk_b, Wv_w, Wv_b, Wo_w, Wo_b):
        import jax, jax.numpy as jnp
        import numpy as np
        B, N, D = (8, 256, 1024)
        H = 8
        HEAD_DIM = D // H
        E = HEAD_DIM // H
        b, n, _ = x.shape
        qk = (x @ Wqk_w.T + Wqk_b).reshape(b, n, H, E, 2)
        q = jnp.transpose(qk[..., 0], (0, 2, 1, 3))
        k = jnp.transpose(qk[..., 1], (0, 2, 1, 3))
        v = (x @ Wv_w.T + Wv_b).reshape(b, n, H, E)
        v = jnp.transpose(v, (0, 2, 1, 3))
        scores = jnp.einsum('bhqd,bhkd->bhqk', q, k)
        attn = jax.nn.softmax(scores, axis=-1) / jnp.asarray(HEAD_DIM ** 0.5, x.dtype)
        out = jnp.einsum('bhsl,bhlv->bhsv', attn, v)
        out = jnp.transpose(out, (0, 2, 1, 3)).reshape(b, n, H * E)
        return out @ Wo_w.T + Wo_b

    def _L0_ffn_ref(x, gate_q, gate_s, up_q, up_s, down_q, down_s):
        import jax, jax.numpy as jnp
        import numpy as np
        H = 1024
        I = 3584
        G = 128

        def dequant(q, s, g=G):
            O, In = q.shape
            return (q.reshape(O, In // g, g).astype(s.dtype) * s[:, :, None]).reshape(O, In)
        Wg = dequant(gate_q, gate_s)
        Wu = dequant(up_q, up_s)
        Wd = dequant(down_q, down_s)
        gate_score = jax.nn.silu(jnp.einsum('bsh,ih->bsi', x, Wg))
        intermediate = gate_score * jnp.einsum('bsh,ih->bsi', x, Wu)
        return jnp.einsum('bsi,hi->bsh', intermediate, Wd)
    h = _L0_tok_ref(x, L0_tok_A, L0_tok_B)
    h = h + _L0_attn_ref(_layernorm(h, axis=-1), L0_attn_Wqk_w, L0_attn_Wqk_b, L0_attn_Wv_w, L0_attn_Wv_b, L0_attn_Wo_w, L0_attn_Wo_b)
    h = h + _L0_ffn_ref(_layernorm(h, axis=-1), L0_ffn_gate_q, L0_ffn_gate_s, L0_ffn_up_q, L0_ffn_up_s, L0_ffn_down_q, L0_ffn_down_s)
    return h

_drawn_inputs = setup_inputs


def setup_inputs(seed=0):
    import zlib

    import numpy as np

    out = dict(_drawn_inputs(seed))
    spreads = {'L0_attn_Wqk_b': (0.0, 0.8), 'L0_attn_Wv_b': (0.0, 2.0), 'L0_attn_Wo_b': (0.0, 0.488)}
    factors = {'L0_attn_Wqk_w': 8.0, 'L0_attn_Wv_w': 8.0, 'L0_attn_Wo_w': 8.0}
    for name, (base, spread) in spreads.items():
        noise = np.random.default_rng([zlib.crc32(name.encode()), seed]).standard_normal(out[name].shape)
        drawn = base * np.exp(spread * noise) if base else spread * noise
        out[name] = jnp.asarray(drawn.astype(out[name].dtype))
    for name, factor in factors.items():
        out[name] = (out[name] * factor).astype(out[name].dtype)
    return out
```

```python
from contextlib import ExitStack

import concourse.bass as bass
from concourse import mybir

ALU = mybir.AluOpType
ACT = mybir.ActivationFunctionType
AX = mybir.AxisListType
F32 = mybir.dt.float32
F16 = mybir.dt.float16
BF16 = mybir.dt.bfloat16
I32 = mybir.dt.int32

P = 128


def lm_tower_kernel(nc, ids, A_T, B_T, wqkv_T, qkv_b, wo_T, wo_b, gu_q, gu_s, dn_q, dn_s, out):
    NT = ids.shape[1]
    R, D = B_T.shape
    HD = wo_T.shape[0]
    H = 8
    E = HD // H
    KD = D // P
    NB = 4
    TB = NT // NB
    S = TB * P
    IT = gu_q.shape[0]
    BI = 2
    NBLK = IT // BI
    HALF = D // 2
    EPS = 1e-5
    TERMS = 6
    KS = TERMS * E
    KX = KS + 3
    XS = 1024.0

    ctx = ExitStack()
    with ctx:
        def sb(name, shape, dt):
            return ctx.enter_context(nc.sbuf_tensor(name, shape, dt))

        def sem(name):
            return ctx.enter_context(nc.semaphore(name))

        hres = sb("hres", [P, NT, D], F32)
        xT = sb("xT", [P, NB, KD, 2, S], F16)
        wgu = sb("wgu", [P, 2, BI, 2, D], F16)
        wdn = sb("wdn", [P, 2, BI, 2, D], F16)
        zT = sb("zT", [P, 2, BI, 2, S], F16)
        gsc = sb("gsc", [P, 2, BI, 2, KD], F32)
        qst = sb("qst", [P, 2, HALF], I32)
        sst = sb("sst", [P, 2, HALF], F32)
        accd = sb("accd", [P, BI, 2, S], F32)
        acca = sb("acca", [P, BI, 2, S], F32)
        tmpa = sb("tmpa", [P, 2, S], F32)
        tnh = sb("tnh", [P, S], F32)
        identf = sb("identf", [P, P], F32)
        identb = sb("identb", [P, P], BF16)
        ids_sb = sb("ids_sb", [P, NT], I32)
        low = sb("low", [P, NT, R], F32)
        lowc = sb("lowc", [P, TB, R], F32)
        lowx = sb("lowx", [P, TB, R + 1], F32)
        st1 = sb("st1", [P, TB, 2, 6], F32)
        mv1 = sb("mv1", [P, TB, 2], F32)
        rs1 = sb("rs1", [P, TB], F32)
        st2 = sb("st2", [P, TB, 2, 6], F32)
        mv2 = sb("mv2", [P, TB, 2], F32)
        rs2 = sb("rs2", [P, TB], F32)
        mhalf = sb("mhalf", [P, TB], F32)
        nmax = sb("nmax", [P, H, TB], F32)
        nres = sb("nres", [P, H, TB], F32)
        nparts = sb("nparts", [P, 3, H, TB], BF16)
        rden = sb("rden", [P, TB, H], F32)
        bmean = sb("bmean", [R, 1], F32)
        Bc = sb("Bc", [P, KD, R], F32)
        smax = sb("smax", [P, 4], F32)
        sall = sb("sall", [P, 4], F32)
        sexp = sb("sexp", [P, 8], I32)
        spow = sb("spow", [P, 8], I32)

        qT = wgu[:, 1, :, :, :].rearrange("p a b c -> p (a b c)").bitcast(BF16)\
            .rearrange("p (h s) -> p h s", h=H)
        kT = wdn[:, 1, :, :, :].rearrange("p a b c -> p (a b c)").bitcast(BF16)\
            .rearrange("p (h s) -> p h s", h=H)
        zflat = zT[:, :, :, :, :].rearrange("p q a b c -> p (q a b c)").bitcast(F32)
        woT = zflat[:, 0:D]
        xs = zflat[:, D:2 * D]
        accf = accd[:, :, :, :].rearrange("p a b c -> p (a b c)")
        BT = accf[0:R, 0:D]
        bo = accf[:, D:2 * D]
        accg = acca[:, :, :, :].rearrange("p a b c -> p (a b c)")
        stacks = accg[:, 0:H * KS].bitcast(BF16)
        qstack = stacks[:, 0:H * KS].rearrange("p (h r e) -> p h r e", h=H, r=TERMS)
        kstack = stacks[:, H * KS:2 * H * KS].rearrange("p (h r e) -> p h r e", h=H, r=TERMS)
        Mqkv = accg[:, 1024:1024 + 3 * HD]
        vaug = tmpa[:, :, :].rearrange("p a b -> p (a b)")[:, 0:TB * H * (E + 1)]\
            .rearrange("p (t h e) -> p t h e", t=TB, h=H)
        last = xT[:, NB - 1, :, :, :].rearrange("p a b c -> p (a b c)").bitcast(F32)
        probs = last.rearrange("p (n k s) -> p n k s", n=2, k=TB)
        wqkv = last[:, 0:KD * 3 * HD].rearrange("p (k n) -> p k n", k=KD)
        lowT = last[0:R, 0:S]
        lowxT = last[0:R + 1, S:2 * S]
        res1 = last[:, 1024:1536].rearrange("p (n c) -> p n c", n=2)
        part = last[:, 1536:2304].bitcast(BF16).rearrange("p (n j c) -> p n j c", n=2, j=3)
        o_sb = last[:, 2304:2304 + TB * HD].rearrange("p (t c) -> p t c", t=TB)
        oT = last[:, 2816:2816 + S]
        BcT = last[0:R, 3072:4096]
        gs_ld = hres[:, NT - 3, 0:NBLK * BI * 2 * KD]
        ds_ld = hres[0:IT, NT - 2, :]

        banks = ctx.enter_context(nc.psum_tensor("banks", [P, 8, 512], F32))

        def bank(i, n=1):
            return banks[:, i, :] if n == 1 else banks[:, i:i + n, :]

        def bankb(i):
            return banks[:, i, :].bitcast(BF16)

        ids_in = sem("ids_in")
        BT_in = sem("BT_in")
        bias_in = sem("bias_in")
        wqkv_in = sem("wqkv_in")
        wo_in = sem("wo_in")
        bo_in = sem("bo_in")
        sall_in = sem("sall_in")
        gsc_in = [sem("gsc_in0"), sem("gsc_in1")]
        low_in = sem("low_in")
        ident_step = sem("ident_step")
        ones_set = sem("ones_set")
        smax_made = sem("smax_made")
        sall_made = sem("sall_made")
        spow_step = sem("spow_step")
        Bc_step = sem("Bc_step")
        BcT_ps = sem("BcT_ps")
        Bc_made = sem("Bc_made")
        M_ps = sem("M_ps")
        M_made = sem("M_made")
        lowc_made = sem("lowc_made")
        lowT_ps = sem("lowT_ps")
        lowT_made = sem("lowT_made")
        h_ps = sem("h_ps")
        h_stats = sem("h_stats")
        h_copied = sem("h_copied")
        bo_added = sem("bo_added")
        dve_step = sem("dve_step")
        waited = sem("waited")
        st2_made = sem("st2_made")
        var1_made = sem("var1_made")
        rstd1_made = sem("rstd1_made")
        var2_made = sem("var2_made")
        rstd2_made = sem("rstd2_made")
        lowx_made = sem("lowx_made")
        lowxT_ps = sem("lowxT_ps")
        lowxT_made = sem("lowxT_made")
        qkv_ps = sem("qkv_ps")
        part1_made = sem("part1_made")
        res1_made = sem("res1_made")
        part2_made = sem("part2_made")
        part3_made = sem("part3_made")
        v_made = sem("v_made")
        qstack_made = sem("qstack_made")
        kstack_made = sem("kstack_made")
        stackT_ps = sem("stackT_ps")
        qT_made = sem("qT_made")
        kT_made = sem("kT_made")
        score_ps = sem("score_ps")
        max_made = sem("max_made")
        nparts_made = sem("nparts_made")
        maxrow_ps = sem("maxrow_ps")
        maxrow_made = sem("maxrow_made")
        scoreT_ps = sem("scoreT_ps")
        probs_made = sem("probs_made")
        pv_ps = sem("pv_ps")
        o_made = sem("o_made")
        oT_ps = sem("oT_ps")
        oT_made = sem("oT_made")
        wo_ps = sem("wo_ps")
        attn_added = sem("attn_added")
        xs_made = sem("xs_made")
        xsT_ps = sem("xsT_ps")
        xhi_made = sem("xhi_made")
        xlo_made = sem("xlo_made")
        q_in = [sem("q_in0"), sem("q_in1")]
        s_in = [sem("s_in0"), sem("s_in1")]
        w_made = sem("w_made")
        whi_made = sem("whi_made")
        wlo_made = sem("wlo_made")
        gu_cast = sem("gu_cast")
        group_ps = sem("group_ps")
        act_evac = sem("act_evac")
        dve_evac = sem("dve_evac")
        pool_added = sem("pool_added")
        merged = sem("merged")
        tanh_made = sem("tanh_made")
        sg_made = sem("sg_made")
        zf_made = sem("zf_made")
        zhi_made = sem("zhi_made")
        zlo_made = sem("zlo_made")
        down_ps = sem("down_ps")
        down_added = sem("down_added")
        out_done = sem("out_done")

        OWNER = "DADDADDADDADADAD"
        ND, NA = OWNER.count("D"), OWNER.count("A")
        GROUPS = []
        for p_, o_ in enumerate(OWNER):
            i_ = OWNER[:p_].count(o_)
            GROUPS.append((o_, i_, i_ % 2, i_ // 2 + (0 if o_ == "D" else ND // 2)))
        RING = 4
        LAG = BI + 1
        PER_BLK = NB * BI
        BODY = 2 * PER_BLK
        SLOTS = NBLK * PER_BLK
        TURNS = SLOTS // BODY - 1
        GU_UNITS = BI * 2 * 2
        DN_UNITS = BI * 2
        UNITS = GU_UNITS + DN_UNITS

        def evac_wait(eng, s, p):
            o, i, _, _ = GROUPS[p]
            eng.wait_ge(dve_evac if o == "D" else act_evac, s * (ND if o == "D" else NA) + i + 1)

        def schedule(eng, slot):
            for s in range(LAG + 1):
                slot(s, s, s // PER_BLK)
            with eng.Fori(0, TURNS) as i:
                for r in range(LAG + 1, LAG + 1 + BODY):
                    slot(i * BODY + r, r, i * 2 + r // PER_BLK)
            for s in range(TURNS * BODY + LAG + 1, SLOTS + LAG + 1):
                slot(s, s, s // PER_BLK)

        def gsc_loads(s, r, B):
            if isinstance(s, int):
                return 16 * (B // 2 + 1)
            return (s - r) // BODY * 16 + 16 * (r // BODY + 1)

        def has_groups(r):
            return r < SLOTS

        def has_z(r):
            return 1 <= r <= SLOTS

        def prefetch(r):
            q = r % PER_BLK
            if r >= SLOTS - PER_BLK:
                return [], []
            return ([2 * q, 2 * q + 1], []) if 2 * q < GU_UNITS else ([], [q - GU_UNITS // 2])

        def gu_unit(par, k):
            return wgu[:, par, k // 4, k // 2 % 2, (k % 2) * HALF:(k % 2 + 1) * HALF]

        def dn_unit(par, d):
            return wdn[:, par, d // 2, :, (d % 2) * HALF:(d % 2 + 1) * HALF]

        block = ctx.enter_context(nc.Block())

        def stand(eng):
            eng.sem_inc(waited, 1)

        @block.sync
        def _(sp):
            sp.dma_start(ids_sb[:, :], ids).then_inc(ids_in, 16)
            sp.dma_start(BT, B_T).then_inc(BT_in, 16)
            sp.dma_start(wqkv, wqkv_T.rearrange("(k p) n -> p k n", p=P)).then_inc(wqkv_in, 16)
            sp.dma_start(Mqkv[R:R + 1, :], qkv_b).then_inc(bias_in, 16)
            sp.dma_start(bo, wo_b.partition_broadcast(P)).then_inc(bo_in, 16)
            sp.dma_start(woT, wo_T).then_inc(wo_in, 16)
            sp.dma_start(gs_ld.rearrange("p (b c) -> p b c", b=NBLK), gu_s.rearrange("b p c -> p b c"))\
                .then_inc(sall_in, 16)
            sp.dma_start(ds_ld, dn_s).then_inc(sall_in, 16)

            def load_block(B):
                first = isinstance(B, int) and B == 0
                for k in range(UNITS):
                    if not first or k >= 2:
                        if 2 <= k < 2 + GU_UNITS:
                            sp.wait_ge(gu_cast, B * GU_UNITS + k - 1)
                            stand(sp)
                        else:
                            sp.wait_ge(w_made, B * DN_UNITS + k - 1 - (GU_UNITS if k >= 2 else 0))
                            stand(sp)
                    if k < GU_UNITS:
                        src = gu_q[B * BI + k // 4, k // 2 % 2]
                    else:
                        d = k - GU_UNITS
                        src = dn_q[B * BI + d // 2]
                    sp.dma_start(qst[:, k % 2, :], src[:, (k % 2) * HALF:(k % 2 + 1) * HALF])\
                        .then_inc(q_in[k % 2], 16)
                    if k >= GU_UNITS:
                        if not first or d >= 2:
                            sp.wait_ge(wlo_made, B * DN_UNITS + d - 1)
                            stand(sp)
                        sp.dma_start(sst[:, d % 2, :], dn_s[B * BI + d // 2, (d % 2) * HALF:(d % 2 + 1) * HALF]
                                     .partition_broadcast(P)).then_inc(s_in[d % 2], 16)

            def load_scales(B, par):
                sp.dma_start(gsc[:, par, :, :, :].rearrange("p a b c -> p (a b c)"), gu_s[B])\
                    .then_inc(gsc_in[par], 16)

            load_scales(0, 0)
            load_scales(1, 1)
            load_block(0)
            with sp.Fori(0, NBLK // 2 - 1) as i:
                for par in range(2):
                    load_block(i * 2 + 1 + par)
                    sp.wait_ge(dve_evac, (i * 2 + par + 1) * (PER_BLK * ND))
                    stand(sp)
                    sp.wait_ge(act_evac, (i * 2 + par + 1) * (PER_BLK * NA))
                    stand(sp)
                    load_scales(i * 2 + par + 2, par)
            load_block(NBLK - 1)

            for t in range(NT):
                sp.wait_ge(down_added, 2 + (NBLK - 1) * NT + t + 1)
                sp.dma_start(out[t * P:(t + 1) * P, :], hres[:, t, :]).then_inc(out_done, 16)
            sp.wait_ge(out_done, 16 * NT)

        @block.gpsimd
        def _(pool):
            pool.memset(identf[:, :], 0.0).then_inc(ident_step, 1)
            pool.memset(identb[:, :], 0.0).then_inc(ident_step, 1)
            pool.wait_ge(ident_step, 2)
            for m in (identf, identb):
                pool.affine_select(out=m[:, :], in_=m[:, :], compare_op=ALU.not_equal, fill=1.0, base=0,
                                   pattern=[[-1, P]], channel_multiplier=1).then_inc(ident_step, 1)
            pool.wait_ge(ids_in, 16)
            for t in range(NT):
                pool.indirect_dma_start(out=low[:, t, :], out_offset=None, in_=A_T,
                                        in_offset=bass.IndirectOffsetOnAxis(ap=ids_sb[:, t:t + 1], axis=0))\
                    .then_inc(low_in, 16)
            pool.memset(lowx[:, :, R:R + 1], 1.0).then_inc(ones_set, 1)
            pool.memset(mhalf[:, :], -0.5).then_inc(ones_set, 1)
            pool.memset(vaug[:, :, :, E:E + 1], 1.0).then_inc(ones_set, 1)
            pool.wait_ge(smax_made, 2)
            pool.partition_all_reduce(sall[:, 0:3], smax[:, 0:3], P, bass.bass_isa.ReduceOp.max)\
                .then_inc(sall_made, 1)
            pool.wait_ge(bo_in, 16)

            pool.wait_ge(ones_set, 4)
            with pool.Fori(0, NB) as b:
                pool.wait_ge(var1_made, b + 1)
                pool.tensor_tensor(rs1[:, :], rs1[:, :], mhalf[:, :], ALU.pow).then_inc(rstd1_made, 1)
                for t in range(TB):
                    pool.wait_ge(h_copied, b * TB + t + 1)
                    pool.tensor_tensor(hres[:, b * TB + t, :], hres[:, b * TB + t, :], bo, ALU.add)\
                        .then_inc(bo_added, 1)
                for t in range(TB):
                    n = b * TB + t
                    pool.wait_ge(res1_made, n + 1)
                    stand(pool)
                    pool.tensor_copy(part[:, t % 2, 1, :], res1[:, t % 2, :]).then_inc(part2_made, 1)
                    pool.wait_ge(part2_made, n + 1)
                    pool.tensor_tensor(part[:, t % 2, 2, :], res1[:, t % 2, :], part[:, t % 2, 1, :],
                                       ALU.subtract).then_inc(part3_made, 1)
                    pool.wait_ge(part3_made, n + 1)
                    pool.wait_ge(stackT_ps, n + 1)
                    stand(pool)

                    def kp(j):
                        return part[:, t % 2, j, HD:2 * HD].rearrange("p (h e) -> p h e", h=H)
                    pool.tensor_copy(kstack[:, :, 1:6:2, :], kp(0).unsqueeze(2).broadcast_to([P, H, 3, E]))
                    pool.tensor_copy(kstack[:, :, 0:5:4, :], kp(1).unsqueeze(2).broadcast_to([P, H, 2, E]))
                    pool.tensor_copy(kstack[:, :, 2, :], kp(2)).then_inc(kstack_made, 1)
                pool.wait_ge(var2_made, b + 1)
                pool.tensor_tensor(rs2[:, :], rs2[:, :], mhalf[:, :], ALU.pow).then_inc(rstd2_made, 1)

            def split_lo(B, par, d):
                pool.wait_ge(whi_made, B * DN_UNITS + d + 1)
                w = dn_unit(par, d)
                pool.tensor_tensor(w[:, 1, :], sst[:, d % 2, :], w[:, 0, :], ALU.subtract)\
                    .then_inc(wlo_made, 1)

            def slot(s, r, B):
                it, pit, pz = r % BI, (r - 1) % BI, (r - 1) // BI % 2

                def add(i):
                    m = i % 2
                    pool.wait_ge(act_evac, s * NA + i + 1)
                    if i >= 4:
                        pool.wait_ge(pool_added, s * (NA - 2) + i - 3)
                    pool.tensor_tensor(acca[:, it, m, :], acca[:, it, m, :], tmpa[:, m, :], ALU.add)\
                        .then_inc(pool_added, 1)

                if has_z(r):
                    for m in range(2):
                        pool.wait_ge(dve_evac, (s - 1) * ND + ND - 1 + m)
                        pool.wait_ge(pool_added, (s - 1) * (NA - 2) + NA - 3 + m)
                        pool.tensor_tensor(accd[:, pit, m, :], accd[:, pit, m, :], acca[:, pit, m, :],
                                           ALU.add).then_inc(merged, 1)
                if has_groups(r):
                    for i in range(2, NA - 1):
                        add(i)
                if has_z(r):
                    pool.wait_ge(zhi_made, s)
                    pool.tensor_tensor(zT[:, pz, pit, 1, :], accd[:, pit, 1, :], zT[:, pz, pit, 0, :],
                                       ALU.subtract).then_inc(zlo_made, 1)
                if has_groups(r):
                    add(NA - 1)
                for d in prefetch(r)[1]:
                    split_lo(B + 1, (r // PER_BLK + 1) % 2, d)

            for d in range(DN_UNITS):
                split_lo(0, 0, d)
            schedule(pool, slot)

        @block.scalar
        def _(act):
            act.wait_ge(BcT_ps, 1)
            act.activation(Bc[:, :, :].rearrange("p k r -> p (k r)"), bank(0)[:, 0:KD * R], ACT.Copy)\
                .then_inc(Bc_made, 1)
            act.wait_ge(M_ps, 1)
            act.activation(Mqkv[0:R, :], bank(1)[0:R, 0:3 * HD], ACT.Copy).then_inc(M_made, 1)

            with act.Fori(0, NB) as b:
                act.wait_ge(lowT_ps, b + 1)
                act.activation(lowT, bank(6)[0:R, :], ACT.Copy).then_inc(lowT_made, 1)
                for t in range(TB):
                    n = b * TB + t
                    act.wait_ge(h_stats, n + 1)
                    act.activation(hres[:, n, :].rearrange("p (a c) -> p a c", a=2), bank(2 * (t % 2), 2),
                                   ACT.Copy, scale=2.0).then_inc(h_copied, 1)
                act.wait_ge(lowxT_ps, b + 1)
                act.activation(lowxT, bank(7)[0:R + 1, :], ACT.Copy).then_inc(lowxT_made, 1)
                for t in range(TB):
                    n = b * TB + t
                    act.wait_ge(qkv_ps, n + 1)
                    if t >= 2:
                        act.wait_ge(qstack_made, n - 1)
                        act.wait_ge(kstack_made, n - 1)
                    act.activation(part[:, t % 2, 0, :], bank(t % 2)[:, 0:2 * HD], ACT.Copy)\
                        .then_inc(part1_made, 1)
                    act.activation(vaug[:, t, :, 0:E], bank(t % 2)[:, 2 * HD:3 * HD]
                                   .rearrange("p (h e) -> p h e", h=H), ACT.Copy).then_inc(v_made, 1)
                    if t >= 1:
                        act.wait_ge(stackT_ps, n + 1)
                        act.activation(kT[0:KS, :, (t - 1) * P:t * P], bankb(5)[0:KS, :]
                                       .rearrange("p (h s) -> p h s", h=H), ACT.Copy).then_inc(kT_made, 1)
                act.wait_ge(stackT_ps, b * TB + TB + 1)
                act.activation(kT[0:KS, :, (TB - 1) * P:TB * P], bankb(5)[0:KS, :]
                               .rearrange("p (h s) -> p h s", h=H), ACT.Copy).then_inc(kT_made, 1)
                for h in range(H):
                    act.wait_ge(maxrow_ps, b * H + h + 1)
                    act.activation(qT[KS:KX, h, :], bank(4 + h % 2)[KS:KX, :], ACT.Copy)\
                        .then_inc(maxrow_made, 1)
                for h in range(H):
                    if h >= 2:
                        act.wait_ge(pv_ps, b * H + h - 1)
                    for j in range(2):
                        act.wait_ge(scoreT_ps, (b * H + h) * 2 + j + 1)
                        act.activation(probs[:, h % 2, 2 * j:2 * j + 2, :], bank(2 * j, 2), ACT.Exp)\
                            .then_inc(probs_made, 1)
                act.wait_ge(oT_ps, b + 1)
                act.activation(oT, bank(4), ACT.Copy).then_inc(oT_made, 1)
                for t in range(TB):
                    for j in range(2):
                        act.wait_ge(xsT_ps, (b * TB + t) * 2 + j + 2)
                        act.activation(xT[:, b, 4 * j:4 * j + 4, 0, t * P:(t + 1) * P],
                                       bank(j).rearrange("p (k s) -> p k s", k=4), ACT.Copy)\
                            .then_inc(xhi_made, 1)

            def cast_gu(B, par, k):
                act.wait_ge(q_in[k % 2], B * (8 * UNITS) + (k // 2 + 1) * 16)
                act.activation(gu_unit(par, k), qst[:, k % 2, :], ACT.Copy).then_inc(gu_cast, 1)

            def split_hi(B, par, d):
                act.wait_ge(w_made, B * DN_UNITS + d + 1)
                act.activation(dn_unit(par, d)[:, 0, :], sst[:, d % 2, :], ACT.Copy).then_inc(whi_made, 1)

            def slot(s, r, B):
                it, pit, pz, par = r % BI, (r - 1) % BI, (r - 1) // BI % 2, r // PER_BLK % 2
                for p, (o, i, m, k) in enumerate(GROUPS):
                    if o == "D" or not has_groups(r):
                        continue
                    if i == 0 and r % PER_BLK == 0:
                        act.wait_ge(gsc_in[par], gsc_loads(s, r, B))
                    act.wait_ge(group_ps, s * (ND + NA) + p + 1)
                    if i < 2:
                        dst = acca[:, it, m, :]
                        if r >= BI:
                            act.wait_ge(merged, s * 2 - 3 + m)
                    else:
                        dst = tmpa[:, m, :]
                        if r >= 1 or i >= 4:
                            act.wait_ge(pool_added, s * (NA - 2) + i - 3)
                    act.activation(dst, bank(p % RING), ACT.Copy, scale=gsc[:, par, it, m, k:k + 1])\
                        .then_inc(act_evac, 1)
                    if i == 2:
                        tanh(s, r)
                    if i == 4:
                        z_hi(s, r)
                if not has_groups(r):
                    tanh(s, r)
                    z_hi(s, r)
                for k in prefetch(r)[0]:
                    cast_gu(B + 1, 1 - par, k)
                for d in prefetch(r)[1]:
                    split_hi(B + 1, 1 - par, d)

            def tanh(s, r):
                if has_z(r):
                    act.wait_ge(merged, s * 2 - 1)
                    if r >= 2:
                        act.wait_ge(zf_made, s - 1)
                    act.activation(tnh[:, :], accd[:, (r - 1) % BI, 0, :], ACT.Tanh, scale=0.5 / XS)\
                        .then_inc(tanh_made, 1)

            def z_hi(s, r):
                if has_z(r):
                    act.wait_ge(zf_made, s)
                    act.activation(zT[:, (r - 1) // BI % 2, (r - 1) % BI, 0, :], accd[:, (r - 1) % BI, 1, :],
                                   ACT.Copy).then_inc(zhi_made, 1)

            for k in range(GU_UNITS):
                cast_gu(0, 0, k)
            for d in range(DN_UNITS):
                split_hi(0, 0, d)
            schedule(act, slot)

        @block.vector
        def _(dve):
            dve.sem_inc(qT_made, 1)
            dve.sem_inc(kT_made, 1)
            dve.sem_inc(xlo_made, 1)
            dve.wait_ge(sall_in, 32)
            dve.memset(smax[:, :], 0.0).then_inc(smax_made, 1)
            dve.wait_ge(smax_made, 1)
            gs_v = gs_ld.rearrange("p (t m k) -> p m t k", t=IT, m=2)
            for m in range(2):
                dve.tensor_reduce(smax[:, m:m + 1], gs_v[:, m], AX.XY, ALU.max, apply_absolute_value=True)
            dve.tensor_reduce(smax[0:IT, 2:3], ds_ld, AX.X, ALU.max, apply_absolute_value=True)\
                .then_inc(smax_made, 1)
            dve.wait_ge(BT_in, 16)
            dve.tensor_reduce(bmean[:, :], BT, AX.X, ALU.add).then_inc(Bc_step, 1)
            dve.wait_ge(Bc_step, 1)
            dve.tensor_scalar(bmean[:, :], bmean[:, :], 1.0 / D, None, ALU.mult).then_inc(Bc_step, 1)
            dve.wait_ge(Bc_step, 2)
            dve.tensor_scalar(BcT, BT, bmean[:, 0:1], None, ALU.subtract).then_inc(Bc_step, 1)
            dve.wait_ge(sall_made, 1)
            dve.tensor_single_scalar(sexp[:, 0:3], sall[:, 0:3].bitcast(I32), 23, ALU.logical_shift_right)\
                .then_inc(spow_step, 1)
            dve.wait_ge(spow_step, 1)
            dve.tensor_scalar(sexp[:, 0:3], sexp[:, 0:3], 64, None, ALU.max).then_inc(spow_step, 1)
            dve.wait_ge(spow_step, 2)
            dve.tensor_scalar(sexp[:, 4:5], sexp[:, 2:3], -1, 265, ALU.mult, ALU.add).then_inc(spow_step, 1)
            dve.tensor_tensor(sexp[:, 6:7], sexp[:, 0:1], sexp[:, 1:2], ALU.add).then_inc(spow_step, 1)
            dve.wait_ge(spow_step, 4)
            dve.tensor_tensor(sexp[:, 7:8], sexp[:, 6:7], sexp[:, 2:3], ALU.add).then_inc(spow_step, 1)
            dve.tensor_scalar(sexp[:, 5:6], sexp[:, 6:7], -1, 347, ALU.mult, ALU.add).then_inc(spow_step, 1)
            dve.wait_ge(spow_step, 6)
            dve.tensor_scalar(sexp[:, 7:8], sexp[:, 7:8], -252, 1, ALU.add, ALU.max).then_inc(spow_step, 1)
            dve.tensor_scalar(sexp[:, 5:6], sexp[:, 5:6], 1, 254, ALU.max, ALU.min).then_inc(spow_step, 1)
            dve.wait_ge(spow_step, 8)
            dve.tensor_scalar(sexp[:, 7:8], sexp[:, 7:8], 254, None, ALU.min).then_inc(spow_step, 1)
            dve.wait_ge(spow_step, 9)
            dve.tensor_single_scalar(spow[:, 4:8], sexp[:, 4:8], 23, ALU.logical_shift_left)\
                .then_inc(spow_step, 1)

            dve.memset(kT[KS:KX, :, :], 1.0).then_inc(ones_set, 1)
            dve.wait_ge(low_in, 16 * NT)
            with dve.Fori(0, NB) as b:
                STEPS = 5
                base = b * STEPS
                dve.tensor_copy(lowc[:, :, :], low[:, bass.ds(b * TB, TB), :]).then_inc(lowc_made, 1)
                for t in range(TB):
                    n = b * TB + t
                    dve.wait_ge(h_ps, n + 1)
                    stand(dve)
                    for j in range(2):
                        i = dve.bn_stats(st1[:, t, j, :], bank(2 * (t % 2) + j))
                    i.then_inc(h_stats, 1)
                dve.wait_ge(h_stats, b * TB + TB)
                stand(dve)
                for t in range(TB):
                    i = dve.bn_aggr(mv1[:, t, :], st1[:, t, :, :].rearrange("p a b -> p (a b)"))
                i.then_inc(dve_step, 1)
                dve.wait_ge(dve_step, base + 1)
                dve.tensor_scalar(rs1[:, :], mv1[:, :, 1], 4.0, EPS, ALU.mult, ALU.add).then_inc(var1_made, 1)
                dve.wait_ge(rstd1_made, b + 1)
                dve.scalar_tensor_tensor(out=lowx[:, :, 0:R], in0=lowc[:, :, :], scalar=2.0,
                                         in1=rs1[:, :].unsqueeze(2).broadcast_to([P, TB, R]),
                                         op0=ALU.mult, op1=ALU.mult).then_inc(lowx_made, 1)
                for t in range(TB):
                    n = b * TB + t
                    dve.wait_ge(part1_made, n + 1)
                    dve.wait_ge(v_made, n + 1)
                    dve.tensor_tensor(res1[:, t % 2, :], bank(t % 2)[:, 0:2 * HD], part[:, t % 2, 0, :],
                                      ALU.subtract).then_inc(res1_made, 1)
                    dve.wait_ge(part3_made, n + 1)
                    dve.wait_ge(stackT_ps, n + 1)

                    def qp(j):
                        return part[:, t % 2, j, 0:HD].rearrange("p (h e) -> p h e", h=H)
                    dve.tensor_copy(qstack[:, :, 0:3, :], qp(0).unsqueeze(2).broadcast_to([P, H, 3, E]))
                    dve.tensor_copy(qstack[:, :, 3:5, :], qp(1).unsqueeze(2).broadcast_to([P, H, 2, E]))
                    dve.tensor_copy(qstack[:, :, 5, :], qp(2)).then_inc(qstack_made, 1)
                    dve.wait_ge(stackT_ps, n + 2)
                    dve.tensor_copy(qT[0:KS, :, t * P:(t + 1) * P], bankb(4)[0:KS, :]
                                    .rearrange("p (h s) -> p h s", h=H)).then_inc(qT_made, 1)
                for h in range(H):
                    for j in range(2):
                        dve.wait_ge(score_ps, (b * H + h) * 2 + j + 1)
                        dve.reduce_max(nmax[:, h, 2 * j:2 * j + 2], bank(2 * j, 2), AX.X, negate=True)\
                            .then_inc(max_made, 1)
                dve.wait_ge(max_made, b * H * 2 + H * 2)
                dve.tensor_copy(nparts[:, 0, :, :], nmax[:, :, :]).then_inc(nparts_made, 1)
                dve.wait_ge(nparts_made, b * 3 + 1)
                dve.tensor_tensor(nres[:, :, :], nmax[:, :, :], nparts[:, 0, :, :], ALU.subtract)\
                    .then_inc(dve_step, 1)
                dve.wait_ge(dve_step, base + 2)
                dve.tensor_copy(nparts[:, 1, :, :], nres[:, :, :]).then_inc(nparts_made, 1)
                dve.wait_ge(nparts_made, b * 3 + 2)
                dve.tensor_tensor(nparts[:, 2, :, :], nres[:, :, :], nparts[:, 1, :, :], ALU.subtract)\
                    .then_inc(nparts_made, 1)
                dve.wait_ge(pv_ps, b * H + H)
                po = bank(6, 2)[:, :, 0:2 * H * (E + 1)].rearrange("p a (t h e) -> p a t h e", t=2, h=H)
                for a in range(2):
                    i = dve.tensor_scalar(rden[:, 2 * a:2 * a + 2, :], po[:, a, :, :, E], float(HD) ** 0.5,
                                          None, ALU.mult)
                i.then_inc(dve_step, 1)
                dve.wait_ge(dve_step, base + 3)
                dve.reciprocal(rden[:, :, :], rden[:, :, :]).then_inc(dve_step, 1)
                dve.wait_ge(dve_step, base + 4)
                for t in range(TB):
                    i = dve.tensor_tensor(o_sb[:, t, :].rearrange("p (h e) -> p h e", h=H),
                                          po[:, t // 2, t % 2, :, 0:E],
                                          rden[:, t, :].unsqueeze(2).broadcast_to([P, H, E]), ALU.mult)
                i.then_inc(o_made, 1)
                for t in range(TB):
                    n = b * TB + t
                    hv = hres[:, n, :].rearrange("p (a c) -> p a c", a=2)
                    dve.wait_ge(wo_ps, n + 1)
                    dve.wait_ge(bo_added, n + 1)
                    dve.tensor_tensor(hv, bank(4 + 2 * (t % 2), 2), hv, ALU.add).then_inc(attn_added, 1)
                    dve.wait_ge(attn_added, n + 1)
                    stand(dve)
                    for j in range(2):
                        i = dve.bn_stats(st2[:, t, j, :], hv[:, j, :])
                    i.then_inc(st2_made, 1)
                    dve.wait_ge(st2_made, n + 1)
                    stand(dve)
                    i = dve.bn_aggr(mv2[:, t, :], st2[:, t, :, :].rearrange("p a b -> p (a b)"))
                i.then_inc(dve_step, 1)
                dve.wait_ge(dve_step, base + 5)
                dve.tensor_scalar(rs2[:, :], mv2[:, :, 1], XS ** -2, EPS * XS ** -2, ALU.mult, ALU.add)\
                    .then_inc(var2_made, 1)
                dve.wait_ge(rstd2_made, b + 1)
                for t in range(TB):
                    n = b * TB + t
                    dve.wait_ge(xsT_ps, n * 2 + 1)
                    dve.tensor_scalar(xs, hres[:, n, :], mv2[:, t, 0:1], rs2[:, t:t + 1], ALU.subtract, ALU.mult)\
                        .then_inc(xs_made, 1)
                    for j in range(2):
                        dve.wait_ge(xhi_made, n * 2 + j + 1)
                        xd = xT[:, b, 4 * j:4 * j + 4, :, t * P:(t + 1) * P]
                        dve.tensor_tensor(xd[:, :, 1, :], bank(j).rearrange("p (k s) -> p k s", k=4),
                                          xd[:, :, 0, :], ALU.subtract).then_inc(xlo_made, 1)

            dve.sem_inc(down_added, 2)

            def dequant(B, par, d):
                dve.wait_ge(q_in[d % 2], B * (8 * UNITS) + 8 * GU_UNITS + (d // 2 + 1) * 16)
                dve.wait_ge(s_in[d % 2], B * (8 * DN_UNITS) + (d // 2 + 1) * 16)
                dve.scalar_tensor_tensor(out=sst[:, d % 2, :], in0=qst[:, d % 2, :],
                                         scalar=spow[:, 4:5].bitcast(F32), in1=sst[:, d % 2, :],
                                         op0=ALU.mult, op1=ALU.mult).then_inc(w_made, 1)

            def down_add(count, r):
                t = (r - LAG) // BI % NB * TB + (r - LAG) % BI * 2
                hv = hres[:, t + 1 if count[1] else t, :].rearrange("p (a c) -> p a c", a=2)
                dve.wait_ge(down_ps, count[0])
                dve.scalar_tensor_tensor(out=hv, in0=bank(4 + 2 * count[1], 2), scalar=spow[:, 7:8].bitcast(F32),
                                         in1=hv, op0=ALU.mult, op1=ALU.add).then_inc(down_added, 1)

            def slot(s, r, B):
                it, pit, par = r % BI, (r - 1) % BI, r // PER_BLK % 2

                def second_tile():
                    if LAG + 1 <= r <= SLOTS + LAG:
                        down_add(((s - LAG) * 2, 1), r - 1)

                def first_tile():
                    if LAG <= r < SLOTS + LAG:
                        down_add(((s - LAG) * 2 + 1, 0), r)

                def z():
                    if has_z(r):
                        dve.wait_ge(tanh_made, s)
                        dve.scalar_tensor_tensor(out=tnh[:, :], in0=tnh[:, :], scalar=1.0,
                                                 in1=accd[:, pit, 0, :], op0=ALU.add, op1=ALU.mult)\
                            .then_inc(sg_made, 1)
                        dve.wait_ge(sg_made, s)
                        dve.wait_ge(merged, s * 2)
                        dve.scalar_tensor_tensor(out=accd[:, pit, 1, :], in0=tnh[:, :],
                                                 scalar=spow[:, 5:6].bitcast(F32), in1=accd[:, pit, 1, :],
                                                 op0=ALU.mult, op1=ALU.mult).then_inc(zf_made, 1)

                if not has_groups(r):
                    second_tile()
                    z()
                    first_tile()
                    return
                for p, (o, i, m, k) in enumerate(GROUPS):
                    if o == "A":
                        continue
                    if i == 0 and r % PER_BLK == 0:
                        dve.wait_ge(gsc_in[par], gsc_loads(s, r, B))
                    acc, sc = accd[:, it, m, :], gsc[:, par, it, m, k:k + 1]
                    dve.wait_ge(group_ps, s * (ND + NA) + p + 1)
                    if i < 2:
                        if r >= BI:
                            dve.wait_ge(zlo_made, s - 1)
                        dve.tensor_scalar(acc, bank(p % RING), sc, None, ALU.mult).then_inc(dve_evac, 1)
                    else:
                        dve.wait_ge(dve_evac, s * ND + i - 1)
                        dve.scalar_tensor_tensor(out=acc, in0=bank(p % RING), scalar=sc, in1=acc,
                                                 op0=ALU.mult, op1=ALU.add).then_inc(dve_evac, 1)
                    if i == 1:
                        second_tile()
                    if i == 5:
                        z()
                    if i == 7:
                        first_tile()
                for d in prefetch(r)[1]:
                    dequant(B + 1, 1 - par, d)

            dve.wait_ge(spow_step, 10)
            for d in range(DN_UNITS):
                dequant(0, 0, d)
            schedule(dve, slot)

        @block.tensor
        def _(pe):
            pe.sem_inc(stackT_ps, 1)
            pe.sem_inc(xsT_ps, 1)
            pe.wait_ge(ident_step, 4)
            pe.wait_ge(Bc_step, 3)
            for k in range(KD):
                i = pe.transpose(bank(0)[:, k * R:(k + 1) * R], BcT[:, k * P:(k + 1) * P], identf[0:R, 0:R])
            i.then_inc(BcT_ps, 1)
            pe.wait_ge(Bc_made, 1)
            pe.wait_ge(wqkv_in, 16)
            for k in range(KD):
                i = pe.matmul(bank(1)[0:R, 0:3 * HD], Bc[:, k, :], wqkv[:, k, :], start=(k == 0),
                              stop=(k == KD - 1))
            i.then_inc(M_ps, 1)
            pe.wait_ge(BT_in, 16)
            pe.wait_ge(bias_in, 16)
            pe.wait_ge(ones_set, 4)
            pe.wait_ge(M_made, 1)
            pe.wait_ge(wo_in, 16)

            with pe.Fori(0, NB) as b:
                pe.wait_ge(lowc_made, b + 1)
                for t in range(TB):
                    i = pe.transpose(bank(6)[0:R, t * P:(t + 1) * P], lowc[:, t, :], identf[:, :])
                i.then_inc(lowT_ps, 1)
                pe.wait_ge(lowT_made, b + 1)
                pe.wait_ge(xlo_made, b * TB * 2 + 1)
                for t in range(TB):
                    if t >= 2:
                        pe.wait_ge(h_stats, b * TB + t - 1)
                        pe.wait_ge(h_copied, b * TB + t - 1)
                    for j in range(2):
                        i = pe.matmul(bank(2 * (t % 2) + j), lowT[:, t * P:(t + 1) * P],
                                      BT[:, j * 512:(j + 1) * 512], start=True, stop=True)
                    i.then_inc(h_ps, 1)
                pe.wait_ge(lowx_made, b + 1)
                for t in range(TB):
                    i = pe.transpose(bank(7)[0:R + 1, t * P:(t + 1) * P], lowx[:, t, :], identf[:, :])
                i.then_inc(lowxT_ps, 1)
                pe.wait_ge(lowxT_made, b + 1)
                pe.wait_ge(h_copied, b * TB + TB)
                for t in range(TB + 1):
                    if t < TB:
                        if t >= 2:
                            pe.wait_ge(v_made, b * TB + t - 1)
                            pe.wait_ge(res1_made, b * TB + t - 1)
                        pe.matmul(bank(t % 2)[:, 0:3 * HD], lowxT[:, t * P:(t + 1) * P], Mqkv[0:R + 1, :],
                                  start=True, stop=True).then_inc(qkv_ps, 1)
                    if t >= 1:
                        n = b * TB + t - 1
                        pe.wait_ge(qstack_made, n + 1)
                        pe.wait_ge(kstack_made, n + 1)
                        pe.wait_ge(qT_made, n + 1)
                        pe.wait_ge(kT_made, n + 1)
                        for j, st in enumerate((qstack, kstack)):
                            for h in range(H):
                                i = pe.transpose(bankb(4 + j)[0:KS, h * P:(h + 1) * P],
                                                 st[:, h, :, :].rearrange("p r e -> p (r e)"), identb[:, :])
                        i.then_inc(stackT_ps, 1)
                pe.wait_ge(qT_made, b * TB + TB + 1)
                pe.wait_ge(kT_made, b * TB + TB + 1)
                for h in range(H):
                    for j in range(2):
                        if h >= 1:
                            pe.wait_ge(max_made, (b * H + h) * 2 + j - 1)
                        for t in range(2):
                            q0 = (2 * j + t) * P
                            i = pe.matmul(bank(2 * j + t), qT[0:KS, h, q0:q0 + P], kT[0:KS, h, :],
                                          start=True, stop=True)
                        i.then_inc(score_ps, 1)
                pe.wait_ge(nparts_made, b * 3 + 3)
                for h in range(H):
                    if h >= 2:
                        pe.wait_ge(maxrow_made, b * H + h - 1)
                    for t in range(TB):
                        i = pe.matmul(bank(4 + h % 2)[KS:KX, t * P:(t + 1) * P], nparts[:, :, h, t],
                                      identb[:, :], start=True, stop=True)
                    i.then_inc(maxrow_ps, 1)

                def scores_t(h):
                    for j in range(2):
                        if h >= 1:
                            pe.wait_ge(probs_made, (b * H + h) * 2 + j - 1)
                        for k in range(2):
                            k0 = (2 * j + k) * P
                            i = pe.matmul(bank(2 * j + k), kT[0:KX, h, k0:k0 + P], qT[0:KX, h, :],
                                          start=True, stop=True)
                        i.then_inc(scoreT_ps, 1)

                def products_v(h):
                    pe.wait_ge(probs_made, (b * H + h) * 2 + 2)
                    for t in range(TB):
                        col = ((t % 2) * H + h) * (E + 1)
                        for k in range(TB):
                            i = pe.matmul(bank(6 + t // 2)[:, col:col + E + 1],
                                          probs[:, h % 2, k, t * P:(t + 1) * P], vaug[:, k, h, :],
                                          start=(k == 0), stop=(k == TB - 1))
                    i.then_inc(pv_ps, 1)

                pe.wait_ge(maxrow_made, b * H + H)
                scores_t(0)
                for h in range(1, H):
                    scores_t(h)
                    products_v(h - 1)
                products_v(H - 1)
                pe.wait_ge(o_made, b + 1)
                for t in range(TB):
                    i = pe.transpose(bank(4)[:, t * P:(t + 1) * P], o_sb[:, t, :], identf[:, :])
                i.then_inc(oT_ps, 1)
                pe.wait_ge(oT_made, b + 1)
                for t in range(TB):
                    if t >= 2:
                        pe.wait_ge(attn_added, b * TB + t - 1)
                    for j in range(2):
                        i = pe.matmul(bank(4 + 2 * (t % 2) + j), oT[:, t * P:(t + 1) * P],
                                      woT[:, j * 512:(j + 1) * 512], start=True, stop=True)
                    i.then_inc(wo_ps, 1)
                for t in range(TB):
                    n = b * TB + t
                    pe.wait_ge(xs_made, n + 1)
                    for j in range(2):
                        if t >= 1:
                            pe.wait_ge(xlo_made, n * 2 + j - 1 + 1)
                        for k in range(4):
                            i = pe.transpose(bank(j)[:, k * P:(k + 1) * P],
                                             xs[:, (4 * j + k) * P:(4 * j + k + 1) * P], identf[:, :])
                        i.then_inc(xsT_ps, 1)

            pe.wait_ge(xlo_made, NT * 2 + 1)
            def slot(s, r, B):
                it, c, par = r % BI, r // BI % NB, r // PER_BLK % 2
                downs = []
                if LAG <= r < SLOTS + LAG:
                    dr = r - LAG
                    zpar, dpar, t0 = dr // BI % 2, dr // PER_BLK % 2, dr % BI * 2
                    downs = [(t, k, zp, wp, j) for t in range(2) for k in range(BI)
                             for zp, wp in ((0, 0), (0, 1), (1, 0)) for j in range(2)]
                    if dr % PER_BLK == 0:
                        pe.wait_ge(wlo_made, B * DN_UNITS + DN_UNITS)
                    if dr % BI == 0:
                        pe.wait_ge(zlo_made, s - 1)
                half = len(downs) // 2

                def down(x):
                    t, k, zp, wp, j = downs[x]
                    if x % half == 0:
                        pe.wait_ge(down_added, (s - LAG) * 2 + t + 1)
                    i = pe.matmul(bank(4 + 2 * t + j), zT[:, zpar, k, zp, (t0 + t) * P:(t0 + t + 1) * P],
                                  wdn[:, dpar, k, wp, j * 512:(j + 1) * 512],
                                  start=(k == 0 and (zp, wp) == (0, 0)),
                                  stop=(k == BI - 1 and (zp, wp) == (1, 0)))
                    if x % half == half - 1:
                        i.then_inc(down_ps, 1)

                for p, (o, _, m, k) in enumerate(GROUPS):
                    n = len(GROUPS)
                    for x in range(len(downs) * p // n, len(downs) * (p + 1) // n):
                        down(x)
                    if not has_groups(r):
                        continue
                    if p == 0 and r % PER_BLK < BI:
                        pe.wait_ge(gu_cast, B * GU_UNITS + (it + 1) * 4)
                    if p >= RING:
                        evac_wait(pe, s, p - RING)
                    elif r >= 1:
                        evac_wait(pe, s - 1, n + p - RING)
                    w = wgu[:, par, it, m, k * P:(k + 1) * P]
                    pe.matmul(bank(p % RING), w, xT[:, c, k, 0, :], start=True, stop=False)
                    pe.matmul(bank(p % RING), w, xT[:, c, k, 1, :], start=False, stop=True)\
                        .then_inc(group_ps, 1)

            schedule(pe, slot)


def kernel(x, L0_tok_A, L0_tok_B, L0_attn_Wqk_w, L0_attn_Wqk_b, L0_attn_Wv_w, L0_attn_Wv_b, L0_attn_Wo_w,
           L0_attn_Wo_b, L0_ffn_gate_q, L0_ffn_gate_s, L0_ffn_up_q, L0_ffn_up_s, L0_ffn_down_q, L0_ffn_down_s):
    import numpy as np
    import concourse.bacc as bacc
    from concourse.bass_utils import run_bass_kernel_spmd

    def arr(a):
        return np.asarray(a)

    nb, seq = x.shape
    D = L0_tok_B.shape[0]
    HD = L0_attn_Wv_w.shape[0]
    wqk = arr(L0_attn_Wqk_w).reshape(HD, 2, D)
    bqk = arr(L0_attn_Wqk_b).reshape(HD, 2)
    wqkv = np.concatenate([wqk[:, 0], wqk[:, 1], arr(L0_attn_Wv_w)], 0).T
    bqkv = np.concatenate([bqk[:, 0], bqk[:, 1], arr(L0_attn_Wv_b)])[None, :]

    def up_tiles(w):
        i, d = w.shape
        return arr(w).reshape(i // P, P, d // P, P).transpose(0, 3, 2, 1).reshape(i // P, P, d)

    def up_scales(s):
        i, g = s.shape
        return arr(s).reshape(i // (2 * P), 2, P, g).transpose(0, 2, 1, 3)

    gu_s = np.stack([up_scales(L0_ffn_gate_s), up_scales(L0_ffn_up_s)], 3)
    arrays = {
        "ids": arr(x).reshape(-1, P).T,
        "A_T": arr(L0_tok_A).T,
        "B_T": arr(L0_tok_B).T,
        "wqkv_T": wqkv,
        "qkv_b": bqkv,
        "wo_T": arr(L0_attn_Wo_w).T,
        "wo_b": arr(L0_attn_Wo_b),
        "gu_q": np.stack([up_tiles(L0_ffn_gate_q), up_tiles(L0_ffn_up_q)], 1),
        "gu_s": gu_s.reshape(gu_s.shape[0], P, -1),
        "dn_q": arr(L0_ffn_down_q).T.reshape(-1, P, D),
        "dn_s": arr(L0_ffn_down_s).T,
    }
    arrays = {k: np.ascontiguousarray(v) for k, v in arrays.items()}
    nc = bacc.Bacc("TRN2", target_bir_lowering=False, num_devices=1)
    args = [nc.dram_tensor(k, v.shape, mybir.dt.from_np(v.dtype), kind="ExternalInput").ap()
            for k, v in arrays.items()]
    out = nc.dram_tensor("out", (nb * seq, D), F32, kind="ExternalOutput").ap()
    lm_tower_kernel(nc, *args, out)
    got = run_bass_kernel_spmd(nc, [arrays], core_ids=[0])
    return got.results[0]["out"].reshape(nb, seq, D)
```

```python
from contextlib import ExitStack

import concourse.bass as bass
from concourse import mybir

ALU = mybir.AluOpType
ACT = mybir.ActivationFunctionType
AX = mybir.AxisListType
F32 = mybir.dt.float32
F16 = mybir.dt.float16
BF16 = mybir.dt.bfloat16
I32 = mybir.dt.int32

P = 128


def lm_tower_kernel(nc, ids, A_T, B_T, wqkv_T, qkv_b, wo_T, wo_b, gu_q, gu_s, dn_q, dn_s, out):
    NT = ids.shape[1]
    R, D = B_T.shape
    HD = wo_T.shape[0]
    H = 8
    E = HD // H
    KD = D // P
    NB = 4
    TB = NT // NB
    S = TB * P
    IT = gu_q.shape[0]
    BI = 2
    NBLK = IT // BI
    HALF = D // 2
    EPS = 1e-5
    TERMS = 6
    KS = TERMS * E
    KX = KS + 3
    EXP_UP = 10.39
    XS = 1024.0

    ctx = ExitStack()
    with ctx:
        def sb(name, shape, dt):
            return ctx.enter_context(nc.sbuf_tensor(name, shape, dt))

        def sem(name):
            return ctx.enter_context(nc.semaphore(name))

        hres = sb("hres", [P, NT, D], F32)
        xT = sb("xT", [P, NB, KD, 2, S], F16)
        wreg = sb("wreg", [P, 2, 2, BI, 2, D], F16)
        wgu, wdn = wreg[:, 0], wreg[:, 1]
        zT = sb("zT", [P, 2, BI, 2, S], F16)
        gsc = sb("gsc", [P, 2, BI, 2, KD], F32)
        qst = sb("qst", [P, 2, HALF], I32)
        sst = sb("sst", [P, 2, HALF], F32)
        sums = sb("sums", [P, 11 * S], F32)
        accd = sums[:, 0:2 * BI * S].rearrange("p (a b c) -> p a b c", a=BI, b=2)
        acca = sums[:, 2 * BI * S:4 * BI * S].rearrange("p (a b c) -> p a b c", a=BI, b=2)
        tmpa = sums[:, 4 * BI * S:(4 * BI + 2) * S].rearrange("p (b c) -> p b c", b=2)
        tnh = sums[:, (4 * BI + 2) * S:(4 * BI + 3) * S]
        oT = sb("oT", [P, 2, P], F32)
        identf = sb("identf", [P, P], F32)
        identb = sb("identb", [P, P], BF16)
        ids_sb = sb("ids_sb", [P, NT], I32)
        low = sb("low", [P, NT, R], F32)
        lowx = sb("lowx", [P, NT, R], F32)
        lres = sb("lres", [P, NT, R], F32)
        lpart = sb("lpart", [P, 2, NT, R], BF16)
        st1 = sb("st1", [P, TB, 2, 6], F32)
        mv1 = sb("mv1", [P, TB, 2], F32)
        rs1 = sb("rs1", [P, NT], F32)
        rs2 = sb("rs2", [P, TB], F32)
        nmean2 = sb("nmean2", [P, TB], F32)
        nmr2 = sb("nmr2", [P, TB], F32)
        mhalf = sb("mhalf", [P, NT], F32)
        nmax = sb("nmax", [P, TB], F32)
        nres = sb("nres", [P, TB], F32)
        nparts = sb("nparts", [P, 2, 3, TB], BF16)
        osum = sb("osum", [P, TB, E], F32)
        rden = sb("rden", [P, TB], F32)
        bmean = sb("bmean", [R, 1], F32)
        Bc = sb("Bc", [P, KD, R], F32)
        smax = sb("smax", [P, 4], F32)
        sall = sb("sall", [P, 4], F32)
        sexp = sb("sexp", [P, 8], I32)
        spow = sb("spow", [P, 8], I32)

        flat = wreg[:, :, :, :, :, :].rearrange("p w q a b c -> p (w q a b c)").bitcast(F32)
        wqkv = flat[:, 0:KD * 3 * HD].rearrange("p (k n) -> p k n", k=KD)
        BT = flat[0:R, 3072:4096]
        BcT = flat[0:R, 4096:5120]
        Bs = flat[:, 6144:6656].bitcast(BF16)
        Ms = flat[:, 6656:6848].bitcast(BF16)
        lowTs = flat[:, 6848:7872].bitcast(BF16)
        part = flat[:, 0:1152].bitcast(BF16).rearrange("p (n j c) -> p n j c", n=2, j=3)
        res1 = flat[:, 1152:1920].rearrange("p (n c) -> p n c", n=2)
        qstack = flat[:, 1920:1920 + H * KX // 2].bitcast(BF16).rearrange("p (h c) -> p h c", h=H)
        kstack = flat[:, 2320:2320 + H * KX // 2].bitcast(BF16).rearrange("p (h c) -> p h c", h=H)
        ex32 = flat[:, 0:4096].rearrange("p (n k s) -> p n k s", n=2, k=TB)
        exhi = flat[:, 4096:6144].bitcast(F16).rearrange("p (n k s) -> p n k s", n=2, k=TB)
        exlo = flat[:, 6144:8192].bitcast(F16).rearrange("p (n k s) -> p n k s", n=2, k=TB)
        zflat = zT[:, :, :, :, :].rearrange("p q a b c -> p (q a b c)").bitcast(F32)
        woT = zflat[:, 0:D]
        bo = zflat[:, D:2 * D]
        lstack = zflat[:, D:D + NT * KX // 2].bitcast(BF16).rearrange("p (n c) -> p n c", n=NT)
        VC = 3 * E + 1
        vend = TB * NB * H * VC // 2
        vparts = sums[:, 0:vend].bitcast(BF16).rearrange("p (t b h c) -> p t b h c", t=TB, b=NB, h=H)
        o_sb = sums[:, vend:vend + NT * HD].rearrange("p (t b c) -> p t b c", t=TB, b=NB)
        o_cur = sums[:, vend + NT * HD:vend + (NT + 2) * HD].rearrange("p (n c) -> p n c", n=2)
        xs = sums[:, 0:2 * D].rearrange("p (n c) -> p n c", n=2)
        vheads = vparts.rearrange("p t b h c -> p t (b h) c")
        xflat = xT[:, :, :, :, :].rearrange("p a b c d -> p (a b c d)").bitcast(BF16)
        qT = xflat[:, 0:NB * H * S].rearrange("p (u s) -> p u s", s=S)
        kT = xflat[:, NB * H * S:2 * NB * H * S].rearrange("p (u s) -> p u s", s=S)
        brow = hres[0:1, NT - 8, 0:6 * HD].rearrange("p (j c) -> p j c", j=2)
        bparts = hres[0:1, NT - 9, :].bitcast(BF16)[:, 0:9 * HD].rearrange("p (j c) -> p j c", j=3)
        Bres = hres[0:R, NT - 4, :]
        Bparts = hres[0:R, NT - 6:NT - 4, :].rearrange("p a c -> p (a c)").bitcast(BF16)[:, 0:3 * D]\
            .rearrange("p (j c) -> p j c", j=3)
        Mf = hres[0:R, NT - 1, 0:3 * HD]
        Mres = hres[0:R, NT - 1, 3 * HD:6 * HD]
        Mparts = hres[0:R, NT - 7, :].bitcast(BF16)[:, 0:9 * HD].rearrange("p (j c) -> p j c", j=3)
        gs_ld = hres[:, NT - 3, 0:NBLK * BI * 2 * KD]
        ds_ld = hres[0:IT, NT - 2, :]

        banks = ctx.enter_context(nc.psum_tensor("banks", [P, 8, 512], F32))

        def bank(i, n=1):
            return banks[:, i, :] if n == 1 else banks[:, i:i + n, :]

        def bankb(i):
            return banks[:, i, :].bitcast(BF16)

        ids_in = sem("ids_in")
        BT_in = sem("BT_in")
        bias_in = sem("bias_in")
        wqkv_in = sem("wqkv_in")
        wo_in = sem("wo_in")
        bo_in = sem("bo_in")
        sall_in = sem("sall_in")
        gsc_in = [sem("gsc_in0"), sem("gsc_in1")]
        low_in = sem("low_in")
        ident_step = sem("ident_step")
        ones_set = sem("ones_set")
        smax_made = sem("smax_made")
        sall_made = sem("sall_made")
        spow_step = sem("spow_step")
        Bc_step = sem("Bc_step")
        BcT_ps = sem("BcT_ps")
        Bc_made = sem("Bc_made")
        M_ps = sem("M_ps")
        chain = sem("chain")
        Bs_in = sem("Bs_in")
        Ms_in = sem("Ms_in")
        lstack_made = sem("lstack_made")
        lstackT_ps = sem("lstackT_ps")
        lowTs_made = sem("lowTs_made")
        h_ps = sem("h_ps")
        h_stats = sem("h_stats")
        h_copied = sem("h_copied")
        bo_added = sem("bo_added")
        dve_step = sem("dve_step")
        waited = sem("waited")
        var1_made = sem("var1_made")
        rstd1_made = sem("rstd1_made")
        var2_made = sem("var2_made")
        rstd2_made = sem("rstd2_made")
        qkv_ps = sem("qkv_ps")
        part1_made = sem("part1_made")
        res1_made = sem("res1_made")
        part2_made = sem("part2_made")
        part3_made = sem("part3_made")
        v_made = sem("v_made")
        stacks_made = sem("stacks_made")
        stackT_ps = sem("stackT_ps")
        qT_made = sem("qT_made")
        kT_made = sem("kT_made")
        score_ps = sem("score_ps")
        max_made = sem("max_made")
        nparts_made = sem("nparts_made")
        nres_made = sem("nres_made")
        maxrow_ps = sem("maxrow_ps")
        maxrow_made = sem("maxrow_made")
        scoreT_ps = sem("scoreT_ps")
        exhi_made = sem("exhi_made")
        exlo_dve = sem("exlo_dve")
        exlo_pool = sem("exlo_pool")
        pv_ps = sem("pv_ps")
        norm_step = sem("norm_step")
        o_made = sem("o_made")
        ocur_made = sem("ocur_made")
        oT_ps = sem("oT_ps")
        oT_made = sem("oT_made")
        wo_ps = sem("wo_ps")
        attn_added = sem("attn_added")
        st2_made = sem("st2_made")
        shift2_made = sem("shift2_made")
        xs_made = sem("xs_made")
        xsT_ps = sem("xsT_ps")
        xhi_made = sem("xhi_made")
        xlo_made = sem("xlo_made")
        q_in = [sem("q_in0"), sem("q_in1")]
        s_in = [sem("s_in0"), sem("s_in1")]
        w_made = sem("w_made")
        whi_made = sem("whi_made")
        wlo_made = sem("wlo_made")
        gu_cast = sem("gu_cast")
        group_ps = sem("group_ps")
        act_evac = sem("act_evac")
        dve_evac = sem("dve_evac")
        pool_added = sem("pool_added")
        merged = sem("merged")
        tanh_made = sem("tanh_made")
        sg_made = sem("sg_made")
        zf_made = sem("zf_made")
        zhi_made = sem("zhi_made")
        zlo_made = sem("zlo_made")
        down_ps = sem("down_ps")
        down_added = sem("down_added")
        out_done = sem("out_done")

        def tiles(eng, slot, head, lag):
            turns = (NT - head) // TB
            for s in range(head):
                slot(s, s, 0)
            with eng.Fori(0, turns) as i:
                for r in range(head, head + TB):
                    slot(i * TB + r, r, i)
            for s in range(head + turns * TB, NT + lag):
                slot(s, s, 0)

        def tile_live(r, lag):
            return lag <= r < NT + lag

        NU = NB * H

        def heads(eng, slot):
            for s in range(4):
                slot(s, s, 0)
            with eng.Fori(0, (NU - 4) // 2) as i:
                for r in (4, 5):
                    slot(i * 2 + r, r, i)
            for s in range(NU, NU + 3):
                slot(s, s, 0)

        def live(r, lag):
            return lag <= r < NU + lag

        OWNER = "DADDADDADDADADAD"
        ND, NA = OWNER.count("D"), OWNER.count("A")
        GROUPS = []
        for p_, o_ in enumerate(OWNER):
            i_ = OWNER[:p_].count(o_)
            GROUPS.append((o_, i_, i_ % 2, i_ // 2 + (0 if o_ == "D" else ND // 2)))
        RING = 4
        LAG = BI + 1
        PER_BLK = NB * BI
        BODY = 2 * PER_BLK
        SLOTS = NBLK * PER_BLK
        TURNS = SLOTS // BODY - 1
        GU_UNITS = BI * 2 * 2
        DN_UNITS = BI * 2
        UNITS = GU_UNITS + DN_UNITS

        def evac_wait(eng, s, p):
            o, i, _, _ = GROUPS[p]
            eng.wait_ge(dve_evac if o == "D" else act_evac, s * (ND if o == "D" else NA) + i + 1)

        def schedule(eng, slot):
            for s in range(LAG + 1):
                slot(s, s, s // PER_BLK)
            with eng.Fori(0, TURNS) as i:
                for r in range(LAG + 1, LAG + 1 + BODY):
                    slot(i * BODY + r, r, i * 2 + r // PER_BLK)
            for s in range(TURNS * BODY + LAG + 1, SLOTS + LAG + 1):
                slot(s, s, s // PER_BLK)

        def gsc_loads(s, r, B):
            if isinstance(s, int):
                return 16 * (B // 2 + 1)
            return (s - r) // BODY * 16 + 16 * (r // BODY + 1)

        def has_groups(r):
            return r < SLOTS

        def has_z(r):
            return 1 <= r <= SLOTS

        def prefetch(r):
            q = r % PER_BLK
            if r >= SLOTS - PER_BLK:
                return [], []
            return ([2 * q, 2 * q + 1], []) if 2 * q < GU_UNITS else ([], [q - GU_UNITS // 2])

        def first_down_units(r):
            return [r - NT] if 0 <= r - NT < DN_UNITS else []

        def gu_unit(par, k):
            return wgu[:, par, k // 4, k // 2 % 2, (k % 2) * HALF:(k % 2 + 1) * HALF]

        def dn_unit(par, d):
            return wdn[:, par, d // 2, :, (d % 2) * HALF:(d % 2 + 1) * HALF]

        block = ctx.enter_context(nc.Block())

        def stand(eng):
            eng.sem_inc(waited, 1)

        @block.sync
        def _(sp):
            sp.dma_start(ids_sb[:, :], ids).then_inc(ids_in, 16)
            sp.dma_start(BT, B_T).then_inc(BT_in, 16)
            sp.dma_start(wqkv, wqkv_T.rearrange("(k p) n -> p k n", p=P)).then_inc(wqkv_in, 16)
            sp.dma_start(brow[:, 0, :], qkv_b).then_inc(bias_in, 16)
            sp.dma_start(gs_ld.rearrange("p (b c) -> p b c", b=NBLK), gu_s.rearrange("b p c -> p b c"))\
                .then_inc(sall_in, 16)
            sp.dma_start(ds_ld, dn_s).then_inc(sall_in, 16)
            sp.dma_start(woT, wo_T).then_inc(wo_in, 16)

            sp.wait_ge(chain, 4)
            for g, j in enumerate((0, 1, 2, 0, 1, 0)):
                sp.dma_start(Bs[g * R:(g + 1) * R, :], Bparts[:, j, :]).then_inc(Bs_in, 16)
            sp.wait_ge(chain, 13)
            for g, j in enumerate((0, 1, 2, 0, 1, 0)):
                sp.dma_start(Ms[g * R:(g + 1) * R, :], Mparts[:, j, :]).then_inc(Ms_in, 16)
            for j in range(3):
                sp.dma_start(Ms[KS + j:KS + j + 1, :], bparts[:, j, :]).then_inc(Ms_in, 16)
            sp.wait_ge(lstackT_ps, 4)
            sp.dma_start(bo, wo_b.partition_broadcast(P)).then_inc(bo_in, 16)

            def load_block(B):
                first = isinstance(B, int) and B == 0
                for k in range(UNITS):
                    if not first or k >= 2:
                        if 2 <= k < 2 + GU_UNITS:
                            sp.wait_ge(gu_cast, B * GU_UNITS + k - 1)
                            stand(sp)
                        else:
                            sp.wait_ge(w_made, B * DN_UNITS + k - 1 - (GU_UNITS if k >= 2 else 0))
                            stand(sp)
                    if k < GU_UNITS:
                        src = gu_q[B * BI + k // 4, k // 2 % 2]
                    else:
                        d = k - GU_UNITS
                        src = dn_q[B * BI + d // 2]
                    sp.dma_start(qst[:, k % 2, :], src[:, (k % 2) * HALF:(k % 2 + 1) * HALF])\
                        .then_inc(q_in[k % 2], 16)
                    if k >= GU_UNITS:
                        if not first or d >= 2:
                            sp.wait_ge(wlo_made, B * DN_UNITS + d - 1)
                            stand(sp)
                        sp.dma_start(sst[:, d % 2, :], dn_s[B * BI + d // 2, (d % 2) * HALF:(d % 2 + 1) * HALF]
                                     .partition_broadcast(P)).then_inc(s_in[d % 2], 16)

            def load_scales(B, par):
                sp.dma_start(gsc[:, par, :, :, :].rearrange("p a b c -> p (a b c)"), gu_s[B])\
                    .then_inc(gsc_in[par], 16)

            load_scales(0, 0)
            load_scales(1, 1)
            load_block(0)
            with sp.Fori(0, NBLK // 2 - 1) as i:
                for par in range(2):
                    load_block(i * 2 + 1 + par)
                    sp.wait_ge(dve_evac, (i * 2 + par + 1) * (PER_BLK * ND))
                    stand(sp)
                    sp.wait_ge(act_evac, (i * 2 + par + 1) * (PER_BLK * NA))
                    stand(sp)
                    load_scales(i * 2 + par + 2, par)
            load_block(NBLK - 1)

            for t in range(NT):
                sp.wait_ge(down_added, 2 + (NBLK - 1) * NT + t + 1)
                sp.dma_start(out[t * P:(t + 1) * P, :], hres[:, t, :]).then_inc(out_done, 16)
            sp.wait_ge(out_done, 16 * NT)

        @block.gpsimd
        def _(pool):
            pool.memset(identf[:, :], 0.0).then_inc(ident_step, 1)
            pool.memset(identb[:, :], 0.0).then_inc(ident_step, 1)
            pool.wait_ge(ident_step, 2)
            for m in (identf, identb):
                pool.affine_select(out=m[:, :], in_=m[:, :], compare_op=ALU.not_equal, fill=1.0, base=0,
                                   pattern=[[-1, P]], channel_multiplier=1).then_inc(ident_step, 1)
            pool.wait_ge(ids_in, 16)
            for t in range(NT):
                pool.indirect_dma_start(out=low[:, t, :], out_offset=None, in_=A_T,
                                        in_offset=bass.IndirectOffsetOnAxis(ap=ids_sb[:, t:t + 1], axis=0))\
                    .then_inc(low_in, 16)
            pool.memset(mhalf[:, :], -0.5).then_inc(ones_set, 1)
            pool.memset(vparts[:, :, :, :, 3 * E:VC].rearrange("p t b h c -> p (t b h) c"), 1.0)\
                .then_inc(ones_set, 1)
            pool.wait_ge(smax_made, 2)
            pool.partition_all_reduce(sall[:, 0:3], smax[:, 0:3], P, bass.bass_isa.ReduceOp.max)\
                .then_inc(sall_made, 1)
            pool.wait_ge(ones_set, 3)
            with pool.Fori(0, NB) as b:
                rb = rs1[:, bass.ds(b * TB, TB)]
                pool.wait_ge(var1_made, b + 1)
                pool.tensor_tensor(rb, rb, mhalf[:, 0:TB], ALU.pow).then_inc(rstd1_made, 1)

            def qkv_slot(s, r, i):
                if tile_live(r, 1):
                    p, t, b = (r - 1) % 2, (r - 1) % TB, i + (r - 1) // TB
                    pool.wait_ge(part2_made, s)
                    pool.tensor_tensor(part[:, p, 2, 0:2 * HD], res1[:, p, 0:2 * HD], part[:, p, 1, 0:2 * HD],
                                       ALU.subtract).then_inc(part3_made, 1)
                    pool.tensor_tensor(vparts[:, t, b, :, 2 * E:3 * E],
                                       res1[:, p, 2 * HD:3 * HD].rearrange("p (h e) -> p h e", h=H),
                                       part[:, p, 1, 2 * HD:3 * HD].rearrange("p (h e) -> p h e", h=H),
                                       ALU.subtract).then_inc(v_made, 1)

            tiles(pool, qkv_slot, 3, 2)
            pool.wait_ge(bo_in, 16)
            pool.wait_ge(h_copied, NT + TB)

            def head_slot(s, r, i):
                if live(r, 2):
                    pool.wait_ge(exhi_made, s * 2 - 3)
                    if r >= 4:
                        pool.wait_ge(pv_ps, s - 3)
                    pool.tensor_tensor(exlo[:, r % 2, 1, :], ex32[:, r % 2, 1, :], exhi[:, r % 2, 1, :],
                                       ALU.subtract)
                    pool.wait_ge(exhi_made, s * 2 - 2)
                    pool.tensor_tensor(exlo[:, r % 2, 2:4, :], ex32[:, r % 2, 2:4, :], exhi[:, r % 2, 2:4, :],
                                       ALU.subtract).then_inc(exlo_pool, 1)
                if live(r, 0) and r % 2 == 0:
                    hv = hres[:, i + r // 2, :]
                    pool.tensor_tensor(hv, hv, bo, ALU.add).then_inc(bo_added, 1)

            heads(pool, head_slot)

            def split_lo(B, par, d):
                pool.wait_ge(whi_made, B * DN_UNITS + d + 1)
                w = dn_unit(par, d)
                pool.tensor_tensor(w[:, 1, :], sst[:, d % 2, :], w[:, 0, :], ALU.subtract)\
                    .then_inc(wlo_made, 1)

            def slot(s, r, B):
                it, pit, pz = r % BI, (r - 1) % BI, (r - 1) // BI % 2

                def add(i):
                    m = i % 2
                    pool.wait_ge(act_evac, s * NA + i + 1)
                    if i >= 4:
                        pool.wait_ge(pool_added, s * (NA - 2) + i - 3)
                    pool.tensor_tensor(acca[:, it, m, :], acca[:, it, m, :], tmpa[:, m, :], ALU.add)\
                        .then_inc(pool_added, 1)

                if has_z(r):
                    for m in range(2):
                        pool.wait_ge(dve_evac, (s - 1) * ND + ND - 1 + m)
                        pool.wait_ge(pool_added, (s - 1) * (NA - 2) + NA - 3 + m)
                        pool.tensor_tensor(accd[:, pit, m, :], accd[:, pit, m, :], acca[:, pit, m, :],
                                           ALU.add).then_inc(merged, 1)
                if has_groups(r):
                    for i in range(2, NA - 1):
                        add(i)
                if has_z(r):
                    pool.wait_ge(zhi_made, s)
                    pool.tensor_tensor(zT[:, pz, pit, 1, :], accd[:, pit, 1, :], zT[:, pz, pit, 0, :],
                                       ALU.subtract).then_inc(zlo_made, 1)
                if has_groups(r):
                    add(NA - 1)
                for d in prefetch(r)[1]:
                    split_lo(B + 1, (r // PER_BLK + 1) % 2, d)

            def norm_slot(s, r, i):
                if tile_live(r, 2):
                    t = (r - 2) % TB
                    pool.wait_ge(var2_made, s - 1)
                    pool.tensor_tensor(rs2[:, t:t + 1], rs2[:, t:t + 1], mhalf[:, 0:1], ALU.pow)\
                        .then_inc(rstd2_made, 1)
                    pool.wait_ge(rstd2_made, s - 1)
                    pool.tensor_tensor(nmr2[:, t:t + 1], nmean2[:, t:t + 1], rs2[:, t:t + 1], ALU.mult)\
                        .then_inc(shift2_made, 1)
                for d in first_down_units(r):
                    split_lo(0, 0, d)

            pool.wait_ge(pv_ps, NU)
            tiles(pool, norm_slot, 5, 4)
            schedule(pool, slot)

        @block.scalar
        def _(act):
            act.wait_ge(BcT_ps, 1)
            act.activation(Bc[:, :, :].rearrange("p k r -> p (k r)"), bank(6)[:, 0:KD * R], ACT.Copy)\
                .then_inc(Bc_made, 1)
            for a in range(2):
                act.wait_ge(lstackT_ps, a + 1)
                act.activation(lowTs[0:KX, a * 1024:(a + 1) * 1024], bankb(4 + a)[0:KX, :], ACT.Copy)\
                    .then_inc(lowTs_made, 1)
            act.sem_inc(h_copied, TB)
            act.wait_ge(Ms_in, 16 * (TERMS + 3))
            with act.Fori(0, NB) as b:
                for t in range(TB):
                    n = b * TB + t
                    act.wait_ge(h_stats, n + 1)
                    act.activation(hres[:, n, :].rearrange("p (a c) -> p a c", a=2), bank(2 * t, 2),
                                   ACT.Copy, scale=2.0).then_inc(h_copied, 1)
            for a in range(2):
                act.wait_ge(lstackT_ps, a + 3)
                act.activation(lowTs[0:KX, a * 1024:(a + 1) * 1024], bankb(4 + a)[0:KX, :], ACT.Copy)\
                    .then_inc(lowTs_made, 1)

            def qkv_slot(s, r, i):
                p = r % 2
                if tile_live(r, 0):
                    if r >= 2:
                        act.wait_ge(stacks_made, s - 1)
                        act.wait_ge(v_made, s - 1)
                    act.wait_ge(qkv_ps, s + 1)
                    act.activation(part[:, p, 0, :], bank(p)[:, 0:3 * HD], ACT.Copy).then_inc(part1_made, 1)
                if tile_live(r, 2):
                    t, b = (r - 2) % TB, i + (r - 2) // TB
                    act.wait_ge(stackT_ps, s - 1)
                    act.activation(kT[0:KX, bass.ds(b * H, H), t * P:(t + 1) * P] if not isinstance(s, int) else
                                   kT[0:KX, b * H:(b + 1) * H, t * P:(t + 1) * P],
                                   bankb(5 + 2 * p)[0:KX, :].rearrange("p (h s) -> p h s", h=H), ACT.Copy)\
                        .then_inc(kT_made, 1)
                if tile_live(r, 0):
                    act.wait_ge(res1_made, s + 1)
                    act.activation(part[:, p, 1, :], res1[:, p, :], ACT.Copy).then_inc(part2_made, 1)

            tiles(act, qkv_slot, 3, 2)

            def head_slot(s, r, i):
                if live(r, 2) and r >= 4:
                    act.wait_ge(exlo_dve, s - 3)
                    act.wait_ge(exlo_pool, s - 3)
                    act.wait_ge(pv_ps, s - 3)
                for j in range(2):
                    if live(r, 2):
                        act.wait_ge(scoreT_ps, s * 2 - 3 + j)
                        act.activation(ex32[:, r % 2, 2 * j:2 * j + 2, :], bank(2 + 2 * j, 2), ACT.Exp)
                        act.activation(exhi[:, r % 2, 2 * j:2 * j + 2, :], bank(2 + 2 * j, 2), ACT.Exp)\
                            .then_inc(exhi_made, 1)
                    if j == 0 and live(r, 1):
                        act.wait_ge(maxrow_ps, s)
                        act.activation(qT[KS:KX, s - 1, :] if isinstance(s, int) else
                                       qT[KS:KX, bass.ds(s - 1, 1), :].rearrange("p a s -> p (a s)"),
                                       bank(6)[KS:KX, :], ACT.Copy).then_inc(maxrow_made, 1)

            heads(act, head_slot)

            def cast_gu(B, par, k):
                act.wait_ge(q_in[k % 2], B * (8 * UNITS) + (k // 2 + 1) * 16)
                act.activation(gu_unit(par, k), qst[:, k % 2, :], ACT.Copy).then_inc(gu_cast, 1)

            def split_hi(B, par, d):
                act.wait_ge(w_made, B * DN_UNITS + d + 1)
                act.activation(dn_unit(par, d)[:, 0, :], sst[:, d % 2, :], ACT.Copy).then_inc(whi_made, 1)

            def slot(s, r, B):
                it, pit, pz, par = r % BI, (r - 1) % BI, (r - 1) // BI % 2, r // PER_BLK % 2
                for p, (o, i, m, k) in enumerate(GROUPS):
                    if o == "D" or not has_groups(r):
                        continue
                    if i == 0 and r % PER_BLK == 0:
                        act.wait_ge(gsc_in[par], gsc_loads(s, r, B))
                    act.wait_ge(group_ps, s * (ND + NA) + p + 1)
                    if i < 2:
                        dst = acca[:, it, m, :]
                        if r >= BI:
                            act.wait_ge(merged, s * 2 - 3 + m)
                    else:
                        dst = tmpa[:, m, :]
                        if r >= 1 or i >= 4:
                            act.wait_ge(pool_added, s * (NA - 2) + i - 3)
                    act.activation(dst, bank(p % RING), ACT.Copy, scale=gsc[:, par, it, m, k:k + 1])\
                        .then_inc(act_evac, 1)
                    if i == 2:
                        tanh(s, r)
                    if i == 4:
                        z_hi(s, r)
                if not has_groups(r):
                    tanh(s, r)
                    z_hi(s, r)
                for k in prefetch(r)[0]:
                    cast_gu(B + 1, 1 - par, k)
                for d in prefetch(r)[1]:
                    split_hi(B + 1, 1 - par, d)

            def tanh(s, r):
                if has_z(r):
                    act.wait_ge(merged, s * 2 - 1)
                    if r >= 2:
                        act.wait_ge(zf_made, s - 1)
                    act.activation(tnh[:, :], accd[:, (r - 1) % BI, 0, :], ACT.Tanh, scale=0.5 / XS)\
                        .then_inc(tanh_made, 1)

            def z_hi(s, r):
                if has_z(r):
                    act.wait_ge(zf_made, s)
                    act.activation(zT[:, (r - 1) // BI % 2, (r - 1) % BI, 0, :], accd[:, (r - 1) % BI, 1, :],
                                   ACT.Copy).then_inc(zhi_made, 1)

            def norm_slot(s, r, i):
                if tile_live(r, 0):
                    if r >= 2:
                        act.wait_ge(wo_ps, s - 1)
                    act.wait_ge(oT_ps, s + 1)
                    act.activation(oT[:, r % 2, :], bank(r % 2)[:, 0:HD], ACT.Copy).then_inc(oT_made, 1)
                if tile_live(r, 2):
                    t, n = (r - 2) % TB, i * TB + (r - 2)
                    if r >= 4:
                        act.wait_ge(xsT_ps, s * 2 - 6)
                    act.wait_ge(shift2_made, s - 1)
                    act.activation(xs[:, r % 2, :], hres[:, n, :], ACT.Identity, scale=rs2[:, t:t + 1],
                                   bias=nmr2[:, t:t + 1]).then_inc(xs_made, 1)
                if tile_live(r, 3):
                    t, b = (r - 3) % TB, i + (r - 3) // TB
                    for j in range(2):
                        act.wait_ge(xsT_ps, s * 2 - 5 + j)
                        act.activation(xT[:, b, 4 * j:4 * j + 4, 0, t * P:(t + 1) * P],
                                       bank(4 + 2 * ((r - 3) % 2) + j).rearrange("p (k s) -> p k s", k=4),
                                       ACT.Copy).then_inc(xhi_made, 1)
                if 2 * r < GU_UNITS:
                    for k in (2 * r, 2 * r + 1):
                        cast_gu(0, 0, k)
                for d in first_down_units(r):
                    split_hi(0, 0, d)

            act.wait_ge(pv_ps, NU)
            act.wait_ge(exlo_pool, NU)
            tiles(act, norm_slot, 5, 4)
            schedule(act, slot)

        @block.vector
        def _(dve):
            done = [0]

            def link(ins):
                done[0] += 1
                ins.then_inc(chain, 1)
                dve.wait_ge(chain, done[0])

            def fill(stack, parts):
                last = None
                for j, (a, c) in enumerate(((0, 3), (3, 5), (5, 6))):
                    last = dve.tensor_copy(stack[:, :, a:c, :],
                                           parts(j).unsqueeze(2).broadcast_to([P, stack.shape[1], c - a, E]))
                return last

            dve.wait_ge(BT_in, 16)
            dve.tensor_reduce(bmean[:, :], BT, AX.X, ALU.add).then_inc(Bc_step, 1)
            dve.wait_ge(Bc_step, 1)
            dve.tensor_scalar(bmean[:, :], bmean[:, :], 1.0 / D, None, ALU.mult).then_inc(Bc_step, 1)
            dve.wait_ge(Bc_step, 2)
            dve.tensor_scalar(BcT, BT, bmean[:, 0:1], None, ALU.subtract).then_inc(Bc_step, 1)

            link(dve.tensor_copy(Bparts[:, 0, :], BT))
            link(dve.tensor_tensor(Bres, BT, Bparts[:, 0, :], ALU.subtract))
            link(dve.tensor_copy(Bparts[:, 1, :], Bres))
            link(dve.tensor_tensor(Bparts[:, 2, :], Bres, Bparts[:, 1, :], ALU.subtract))

            dve.wait_ge(bias_in, 16)
            link(dve.tensor_copy(bparts[:, 0, :], brow[:, 0, :]))
            link(dve.tensor_tensor(brow[:, 1, :], brow[:, 0, :], bparts[:, 0, :], ALU.subtract))
            link(dve.tensor_copy(bparts[:, 1, :], brow[:, 1, :]))
            link(dve.tensor_tensor(bparts[:, 2, :], brow[:, 1, :], bparts[:, 1, :], ALU.subtract))

            dve.wait_ge(sall_in, 32)
            dve.memset(smax[:, :], 0.0).then_inc(smax_made, 1)
            dve.wait_ge(smax_made, 1)
            gs_v = gs_ld.rearrange("p (t m k) -> p m t k", t=IT, m=2)
            for m in range(2):
                dve.tensor_reduce(smax[:, m:m + 1], gs_v[:, m], AX.XY, ALU.max, apply_absolute_value=True)
            dve.tensor_reduce(smax[0:IT, 2:3], ds_ld, AX.X, ALU.max, apply_absolute_value=True)\
                .then_inc(smax_made, 1)

            dve.wait_ge(M_ps, 1)
            link(dve.tensor_copy(Mf, bank(7)[0:R, 0:3 * HD]))
            link(dve.tensor_copy(Mparts[:, 0, :], Mf))
            link(dve.tensor_tensor(Mres, Mf, Mparts[:, 0, :], ALU.subtract))
            link(dve.tensor_copy(Mparts[:, 1, :], Mres))
            link(dve.tensor_tensor(Mparts[:, 2, :], Mres, Mparts[:, 1, :], ALU.subtract))
            dve.memset(kstack[:, :, KS:KX], 1.0)
            dve.memset(lstack[:, :, KS:KX], 1.0).then_inc(ones_set, 1)

            def low_stack(src):
                lv = lstack[:, :, 0:KS].rearrange("p n (r e) -> p n r e", r=TERMS)
                link(dve.tensor_copy(lpart[:, 0], src))
                link(dve.tensor_tensor(lres[:, :, :], src, lpart[:, 0], ALU.subtract))
                link(dve.tensor_copy(lpart[:, 1], lres[:, :, :]))
                for a, c, j in ((0, 3, 0), (3, 5, 1)):
                    dve.tensor_copy(lv[:, :, a:c, :], lpart[:, j].unsqueeze(2).broadcast_to([P, NT, c - a, R]))
                dve.tensor_tensor(lv[:, :, 5, :], lres[:, :, :], lpart[:, 1], ALU.subtract)\
                    .then_inc(lstack_made, 1)

            dve.wait_ge(low_in, 16 * NT)
            low_stack(low[:, :, :])

            dve.wait_ge(sall_made, 1)
            dve.tensor_single_scalar(sexp[:, 0:3], sall[:, 0:3].bitcast(I32), 23, ALU.logical_shift_right)\
                .then_inc(spow_step, 1)
            dve.wait_ge(spow_step, 1)
            dve.tensor_scalar(sexp[:, 0:3], sexp[:, 0:3], 64, None, ALU.max).then_inc(spow_step, 1)
            dve.wait_ge(spow_step, 2)
            dve.tensor_scalar(sexp[:, 4:5], sexp[:, 2:3], -1, 265, ALU.mult, ALU.add).then_inc(spow_step, 1)
            dve.tensor_tensor(sexp[:, 6:7], sexp[:, 0:1], sexp[:, 1:2], ALU.add).then_inc(spow_step, 1)
            dve.wait_ge(spow_step, 4)
            dve.tensor_tensor(sexp[:, 7:8], sexp[:, 6:7], sexp[:, 2:3], ALU.add).then_inc(spow_step, 1)
            dve.tensor_scalar(sexp[:, 5:6], sexp[:, 6:7], -1, 347, ALU.mult, ALU.add).then_inc(spow_step, 1)
            dve.wait_ge(spow_step, 6)
            dve.tensor_scalar(sexp[:, 7:8], sexp[:, 7:8], -252, 1, ALU.add, ALU.max).then_inc(spow_step, 1)
            dve.tensor_scalar(sexp[:, 5:6], sexp[:, 5:6], 1, 254, ALU.max, ALU.min).then_inc(spow_step, 1)
            dve.wait_ge(spow_step, 8)
            dve.tensor_scalar(sexp[:, 7:8], sexp[:, 7:8], 254, None, ALU.min).then_inc(spow_step, 1)
            dve.wait_ge(spow_step, 9)
            dve.tensor_single_scalar(spow[:, 4:8], sexp[:, 4:8], 23, ALU.logical_shift_left)\
                .then_inc(spow_step, 1)

            with dve.Fori(0, NB) as b:
                for t in range(TB):
                    dve.wait_ge(h_ps, b * TB + t + 1)
                    stand(dve)
                    for j in range(2):
                        i = dve.bn_stats(st1[:, t, j, :], bank(2 * t + j))
                    i.then_inc(h_stats, 1)
                dve.wait_ge(h_stats, b * TB + TB)
                stand(dve)
                for t in range(TB):
                    i = dve.bn_aggr(mv1[:, t, :], st1[:, t, :, :].rearrange("p a b -> p (a b)"))
                i.then_inc(dve_step, 1)
                dve.wait_ge(dve_step, b + 1)
                dve.tensor_scalar(rs1[:, bass.ds(b * TB, TB)], mv1[:, :, 1], 4.0, EPS, ALU.mult, ALU.add)\
                    .then_inc(var1_made, 1)
            dve.wait_ge(rstd1_made, NB)
            dve.wait_ge(lstackT_ps, 2)
            link(dve.scalar_tensor_tensor(out=lowx[:, :, :], in0=low[:, :, :], scalar=2.0,
                                          in1=rs1[:, :].unsqueeze(2).broadcast_to([P, NT, R]),
                                          op0=ALU.mult, op1=ALU.mult))
            low_stack(lowx[:, :, :])

            def qkv_slot(s, r, i):
                if tile_live(r, 0):
                    p = r % 2
                    if r >= 2:
                        dve.wait_ge(v_made, s - 1)
                    dve.wait_ge(part1_made, s + 1)
                    dve.tensor_tensor(res1[:, p, :], bank(p)[:, 0:3 * HD], part[:, p, 0, :],
                                      ALU.subtract).then_inc(res1_made, 1)
                if tile_live(r, 2):
                    t, b = (r - 2) % TB, i + (r - 2) // TB
                    dve.wait_ge(stackT_ps, s - 1)
                    dve.tensor_copy(qT[0:KS, bass.ds(b * H, H), t * P:(t + 1) * P] if not isinstance(s, int) else
                                    qT[0:KS, b * H:(b + 1) * H, t * P:(t + 1) * P],
                                    bankb(4 + 2 * (r % 2))[0:KS, :].rearrange("p (h s) -> p h s", h=H))\
                        .then_inc(qT_made, 1)
                if tile_live(r, 1):
                    p, t, b = (r - 1) % 2, (r - 1) % TB, i + (r - 1) // TB
                    dve.wait_ge(part3_made, s)
                    if r >= 2:
                        dve.wait_ge(stackT_ps, s - 1)
                    stand(dve)
                    qs = qstack[:, :, 0:KS].rearrange("p h (r e) -> p h r e", r=TERMS)
                    ks = kstack[:, :, 0:KS].rearrange("p h (r e) -> p h r e", r=TERMS)

                    def pt(j, x):
                        return part[:, p, j, x * HD:(x + 1) * HD].rearrange("p (h e) -> p h e", h=H)
                    fill(qs, lambda j: pt(j, 0))
                    dve.tensor_copy(ks[:, :, 0:6:3, :], pt(0, 1).unsqueeze(2).broadcast_to([P, H, 2, E]))
                    dve.tensor_copy(ks[:, :, 5, :], pt(0, 1))
                    dve.tensor_copy(ks[:, :, 1:5:3, :], pt(1, 1).unsqueeze(2).broadcast_to([P, H, 2, E]))
                    dve.tensor_copy(ks[:, :, 2, :], pt(2, 1))
                    dve.tensor_copy(vparts[:, t, b, :, 0:E], pt(0, 2))
                    dve.tensor_copy(vparts[:, t, b, :, E:2 * E], pt(1, 2)).then_inc(stacks_made, 1)

            tiles(dve, qkv_slot, 3, 2)

            def head_slot(s, r, i):
                def maxima(j):
                    dve.wait_ge(score_ps, s * 2 + j + 1)
                    dve.reduce_max(nmax[:, 2 * j:2 * j + 2], bank(0, 2), AX.X, negate=True).then_inc(max_made, 1)

                if live(r, 0):
                    maxima(0)
                if live(r, 2):
                    dve.wait_ge(exhi_made, s * 2 - 3)
                    if r >= 4:
                        dve.wait_ge(pv_ps, s - 3)
                    dve.tensor_tensor(exlo[:, r % 2, 0, :], ex32[:, r % 2, 0, :], exhi[:, r % 2, 0, :],
                                      ALU.subtract).then_inc(exlo_dve, 1)
                if live(r, 3):
                    po = bank(7)[:, 0:TB * VC].rearrange("p (t c) -> p t c", t=TB)
                    dve.wait_ge(pv_ps, s - 2)
                    dve.tensor_scalar(rden[:, :], po[:, :, 3 * E], float(HD) ** 0.5, None, ALU.mult)\
                        .then_inc(norm_step, 1)
                    dve.tensor_reduce(osum[:, :, :], po[:, :, 0:3 * E].rearrange("p t (j e) -> p t e j", j=3),
                                      AX.X, ALU.add)
                    dve.wait_ge(norm_step, s * 2 - 5)
                    dve.reciprocal(rden[:, :], rden[:, :]).then_inc(norm_step, 1)
                    dve.wait_ge(norm_step, s * 2 - 4)
                    ov = o_sb.rearrange("p t b c -> p t (b c)")
                    dve.tensor_tensor(ov[:, :, bass.ds((s - 3) * E, E)], osum[:, :, :],
                                      rden[:, :].unsqueeze(2).broadcast_to([P, TB, E]), ALU.mult)\
                        .then_inc(o_made, 1)
                if live(r, 0):
                    maxima(1)
                    np_ = nparts[:, r % 2]
                    dve.wait_ge(max_made, s * 2 + 2)
                    if r >= 2:
                        dve.wait_ge(maxrow_ps, s - 1)
                    dve.tensor_scalar(nmax[:, :], nmax[:, :], EXP_UP, None, ALU.add).then_inc(nres_made, 1)
                    dve.wait_ge(nres_made, s * 3 + 1)
                    dve.tensor_copy(np_[:, 0, :], nmax[:, :]).then_inc(nparts_made, 1)
                    dve.wait_ge(nparts_made, s * 3 + 1)
                    dve.tensor_tensor(nres[:, :], nmax[:, :], np_[:, 0, :], ALU.subtract).then_inc(nres_made, 1)
                    dve.wait_ge(nres_made, s * 3 + 2)
                    dve.tensor_copy(np_[:, 1, :], nres[:, :]).then_inc(nparts_made, 1)
                    dve.wait_ge(nparts_made, s * 3 + 2)
                    dve.tensor_tensor(np_[:, 2, :], nres[:, :], np_[:, 1, :], ALU.subtract)\
                        .then_inc(nparts_made, 1)
                    dve.sem_inc(nres_made, 1)

            heads(dve, head_slot)

            def norm_slot(s, r, i):
                if tile_live(r, 0):
                    if r >= 2:
                        dve.wait_ge(oT_ps, s - 1)
                    dve.tensor_copy(o_cur[:, r % 2, :], o_sb[:, r % TB, i + r // TB, :]).then_inc(ocur_made, 1)
                if tile_live(r, 1):
                    t, n = (r - 1) % TB, i * TB + (r - 1)
                    hv = hres[:, n, :].rearrange("p (a c) -> p a c", a=2)
                    dve.wait_ge(wo_ps, s)
                    dve.tensor_tensor(hv, bank(2, 2), hv, ALU.add).then_inc(attn_added, 1)
                    dve.wait_ge(attn_added, s)
                    stand(dve)
                    for j in range(2):
                        x = dve.bn_stats(st1[:, t, j, :], hv[:, j, :])
                    x.then_inc(st2_made, 1)
                    dve.wait_ge(st2_made, s)
                    stand(dve)
                    dve.bn_aggr(mv1[:, t, :], st1[:, t, :, :].rearrange("p a b -> p (a b)")).then_inc(dve_step, 1)
                    dve.wait_ge(dve_step, s + NB)
                    dve.tensor_scalar(nmean2[:, t:t + 1], mv1[:, t, 0:1], -1.0, None, ALU.mult)
                    dve.tensor_scalar(rs2[:, t:t + 1], mv1[:, t, 1:2], XS ** -2, EPS * XS ** -2, ALU.mult, ALU.add)\
                        .then_inc(var2_made, 1)
                if tile_live(r, 3):
                    t, b = (r - 3) % TB, i + (r - 3) // TB
                    for j in range(2):
                        dve.wait_ge(xhi_made, s * 2 - 5 + j)
                        xd = xT[:, b, 4 * j:4 * j + 4, :, t * P:(t + 1) * P]
                        dve.tensor_tensor(xd[:, :, 1, :], bank(4 + 2 * ((r - 3) % 2) + j)
                                          .rearrange("p (k s) -> p k s", k=4), xd[:, :, 0, :], ALU.subtract)\
                            .then_inc(xlo_made, 1)
                for d in first_down_units(r):
                    dequant(0, 0, d)

            def dequant(B, par, d):
                dve.wait_ge(q_in[d % 2], B * (8 * UNITS) + 8 * GU_UNITS + (d // 2 + 1) * 16)
                dve.wait_ge(s_in[d % 2], B * (8 * DN_UNITS) + (d // 2 + 1) * 16)
                dve.scalar_tensor_tensor(out=sst[:, d % 2, :], in0=qst[:, d % 2, :],
                                         scalar=spow[:, 4:5].bitcast(F32), in1=sst[:, d % 2, :],
                                         op0=ALU.mult, op1=ALU.mult).then_inc(w_made, 1)

            dve.wait_ge(o_made, NU)
            dve.wait_ge(bo_added, NT)
            tiles(dve, norm_slot, 5, 4)

            dve.sem_inc(down_added, 2)

            def down_add(count, r):
                t = (r - LAG) // BI % NB * TB + (r - LAG) % BI * 2
                hv = hres[:, t + 1 if count[1] else t, :].rearrange("p (a c) -> p a c", a=2)
                dve.wait_ge(down_ps, count[0])
                dve.scalar_tensor_tensor(out=hv, in0=bank(4 + 2 * count[1], 2), scalar=spow[:, 7:8].bitcast(F32),
                                         in1=hv, op0=ALU.mult, op1=ALU.add).then_inc(down_added, 1)

            def slot(s, r, B):
                it, pit, par = r % BI, (r - 1) % BI, r // PER_BLK % 2

                def second_tile():
                    if LAG + 1 <= r <= SLOTS + LAG:
                        down_add(((s - LAG) * 2, 1), r - 1)

                def first_tile():
                    if LAG <= r < SLOTS + LAG:
                        down_add(((s - LAG) * 2 + 1, 0), r)

                def z():
                    if has_z(r):
                        dve.wait_ge(tanh_made, s)
                        dve.scalar_tensor_tensor(out=tnh[:, :], in0=tnh[:, :], scalar=1.0,
                                                 in1=accd[:, pit, 0, :], op0=ALU.add, op1=ALU.mult)\
                            .then_inc(sg_made, 1)
                        dve.wait_ge(sg_made, s)
                        dve.wait_ge(merged, s * 2)
                        dve.scalar_tensor_tensor(out=accd[:, pit, 1, :], in0=tnh[:, :],
                                                 scalar=spow[:, 5:6].bitcast(F32), in1=accd[:, pit, 1, :],
                                                 op0=ALU.mult, op1=ALU.mult).then_inc(zf_made, 1)

                if not has_groups(r):
                    second_tile()
                    z()
                    first_tile()
                    return
                for p, (o, i, m, k) in enumerate(GROUPS):
                    if o == "A":
                        continue
                    if i == 0 and r % PER_BLK == 0:
                        dve.wait_ge(gsc_in[par], gsc_loads(s, r, B))
                    acc, sc = accd[:, it, m, :], gsc[:, par, it, m, k:k + 1]
                    dve.wait_ge(group_ps, s * (ND + NA) + p + 1)
                    if i < 2:
                        if r >= BI:
                            dve.wait_ge(zlo_made, s - 1)
                        dve.tensor_scalar(acc, bank(p % RING), sc, None, ALU.mult).then_inc(dve_evac, 1)
                    else:
                        dve.wait_ge(dve_evac, s * ND + i - 1)
                        dve.scalar_tensor_tensor(out=acc, in0=bank(p % RING), scalar=sc, in1=acc,
                                                 op0=ALU.mult, op1=ALU.add).then_inc(dve_evac, 1)
                    if i == 1:
                        second_tile()
                    if i == 5:
                        z()
                    if i == 7:
                        first_tile()
                for d in prefetch(r)[1]:
                    dequant(B + 1, 1 - par, d)

            schedule(dve, slot)

        @block.tensor
        def _(pe):
            pe.wait_ge(ident_step, 4)
            pe.wait_ge(Bc_step, 3)
            for k in range(KD):
                i = pe.transpose(bank(6)[:, k * R:(k + 1) * R], BcT[:, k * P:(k + 1) * P], identf[0:R, 0:R])
            i.then_inc(BcT_ps, 1)
            pe.wait_ge(Bc_made, 1)
            pe.wait_ge(wqkv_in, 16)
            for k in range(KD):
                i = pe.matmul(bank(7)[0:R, 0:3 * HD], Bc[:, k, :], wqkv[:, k, :], start=(k == 0),
                              stop=(k == KD - 1))
            i.then_inc(M_ps, 1)

            def transpose_low(count):
                pe.wait_ge(lstack_made, count)
                for n in range(NT):
                    i = pe.transpose(bankb(4 + n // 8)[0:KX, n % 8 * P:(n % 8 + 1) * P], lstack[:, n, :],
                                     identb[:, :])
                    if n % 8 == 7:
                        i.then_inc(lstackT_ps, 1)
                pe.wait_ge(lowTs_made, 2 * count)

            pe.wait_ge(ones_set, 3)
            transpose_low(1)
            pe.wait_ge(Bs_in, 16 * TERMS)
            with pe.Fori(0, NB) as b:
                for t in range(TB):
                    n = b * TB + t
                    pe.wait_ge(h_copied, n + 1)
                    for j in range(2):
                        i = pe.matmul(bank(2 * t + j), lowTs[0:KS, bass.ds(n * P, P)],
                                      Bs[0:KS, j * 512:(j + 1) * 512], start=True, stop=True)
                    i.then_inc(h_ps, 1)
            pe.wait_ge(h_copied, NT + TB)
            transpose_low(2)
            pe.wait_ge(Ms_in, 16 * (TERMS + 3))
            def qkv_slot(s, r, i):
                if tile_live(r, 0):
                    if r >= 2:
                        pe.wait_ge(res1_made, s - 1)
                    pe.matmul(bank(r % 2)[:, 0:3 * HD], lowTs[0:KX, bass.ds(s * P, P)] if not isinstance(s, int) else
                              lowTs[0:KX, s * P:(s + 1) * P], Ms[0:KX, :], start=True, stop=True)\
                        .then_inc(qkv_ps, 1)
                if tile_live(r, 1):
                    pe.wait_ge(stacks_made, s)
                    if r >= 3:
                        pe.wait_ge(qT_made, s - 2)
                        pe.wait_ge(kT_made, s - 2)
                    for j, (st, rows) in enumerate(((qstack, KS), (kstack, KX))):
                        for h in range(H):
                            x = pe.transpose(bankb(4 + 2 * ((r - 1) % 2) + j)[0:rows, h * P:(h + 1) * P],
                                             st[:, h, 0:rows], identb[:, :])
                    x.then_inc(stackT_ps, 1)

            tiles(pe, qkv_slot, 3, 2)
            pe.wait_ge(qT_made, NT)
            pe.wait_ge(kT_made, NT)
            pe.wait_ge(v_made, NT)

            def head_slot(s, r, i):
                def scores(j):
                    if live(r, 0):
                        if r or j:
                            pe.wait_ge(max_made, s * 2 + j)
                        for t in range(2):
                            x = pe.matmul(bank(t), qT[0:KS, s, (2 * j + t) * P:(2 * j + t + 1) * P],
                                          kT[0:KS, s, :], start=True, stop=True)
                        x.then_inc(score_ps, 1)

                def scores_t(j):
                    if live(r, 2):
                        if j == 0:
                            pe.wait_ge(maxrow_made, s - 1)
                        if r >= 3:
                            pe.wait_ge(exhi_made, s * 2 - 5 + j)
                        for k in range(2):
                            x = pe.matmul(bank(2 + 2 * j + k), kT[0:KX, s - 2, (2 * j + k) * P:(2 * j + k + 1) * P],
                                          qT[0:KX, s - 2, :], start=True, stop=True)
                        x.then_inc(scoreT_ps, 1)

                scores_t(0)
                scores(0)
                scores_t(1)
                if live(r, 1):
                    pe.wait_ge(nparts_made, s * 3)
                    for t in range(TB):
                        x = pe.matmul(bank(6)[KS:KX, t * P:(t + 1) * P], nparts[:, (r - 1) % 2, :, t],
                                      identb[:, :], start=True, stop=True)
                    x.then_inc(maxrow_ps, 1)
                if live(r, 3):
                    pe.wait_ge(exlo_dve, s - 2)
                    pe.wait_ge(exlo_pool, s - 2)
                    if r >= 4:
                        pe.wait_ge(o_made, s - 3)
                    for t in range(TB):
                        for k in range(TB):
                            for part_, ex in enumerate((exhi, exlo)):
                                x = pe.matmul(bank(7)[:, t * VC:(t + 1) * VC],
                                              ex[:, (r - 3) % 2, k, t * P:(t + 1) * P], vheads[:, k, s - 3, :],
                                              start=(k == 0 and part_ == 0), stop=(k == TB - 1 and part_ == 1))
                    x.then_inc(pv_ps, 1)
                scores(1)

            heads(pe, head_slot)

            def norm_slot(s, r, i):
                if tile_live(r, 1):
                    p = (r - 1) % 2
                    pe.wait_ge(oT_made, s)
                    if r >= 2:
                        pe.wait_ge(attn_added, s - 1)
                    for j in range(2):
                        x = pe.matmul(bank(2 + j), oT[:, p, :], woT[:, j * 512:(j + 1) * 512],
                                      start=True, stop=True)
                    x.then_inc(wo_ps, 1)
                if tile_live(r, 0):
                    pe.wait_ge(ocur_made, s + 1)
                    pe.transpose(bank(r % 2)[:, 0:HD], o_cur[:, r % 2, :], identf[:, :]).then_inc(oT_ps, 1)
                if tile_live(r, 3):
                    p = (r - 3) % 2
                    pe.wait_ge(xs_made, s - 2)
                    for j in range(2):
                        if r >= 5:
                            pe.wait_ge(xlo_made, s * 2 - 9 + j)
                        for k in range(4):
                            x = pe.transpose(bank(4 + 2 * p + j)[:, k * P:(k + 1) * P],
                                             xs[:, p, (4 * j + k) * P:(4 * j + k + 1) * P], identf[:, :])
                        x.then_inc(xsT_ps, 1)

            pe.wait_ge(wo_in, 16)
            pe.wait_ge(exhi_made, NU * 2)
            tiles(pe, norm_slot, 5, 4)
            pe.wait_ge(xlo_made, NT * 2)

            def slot(s, r, B):
                it, c, par = r % BI, r // BI % NB, r // PER_BLK % 2
                downs = []
                if LAG <= r < SLOTS + LAG:
                    dr = r - LAG
                    zpar, dpar, t0 = dr // BI % 2, dr // PER_BLK % 2, dr % BI * 2
                    downs = [(t, k, zp, wp, j) for t in range(2) for k in range(BI)
                             for zp, wp in ((0, 0), (0, 1), (1, 0)) for j in range(2)]
                    if dr % PER_BLK == 0:
                        pe.wait_ge(wlo_made, B * DN_UNITS + DN_UNITS)
                    if dr % BI == 0:
                        pe.wait_ge(zlo_made, s - 1)
                half = len(downs) // 2

                def down(x):
                    t, k, zp, wp, j = downs[x]
                    if x % half == 0:
                        pe.wait_ge(down_added, (s - LAG) * 2 + t + 1)
                    i = pe.matmul(bank(4 + 2 * t + j), zT[:, zpar, k, zp, (t0 + t) * P:(t0 + t + 1) * P],
                                  wdn[:, dpar, k, wp, j * 512:(j + 1) * 512],
                                  start=(k == 0 and (zp, wp) == (0, 0)),
                                  stop=(k == BI - 1 and (zp, wp) == (1, 0)))
                    if x % half == half - 1:
                        i.then_inc(down_ps, 1)

                for p, (o, _, m, k) in enumerate(GROUPS):
                    n = len(GROUPS)
                    for x in range(len(downs) * p // n, len(downs) * (p + 1) // n):
                        down(x)
                    if not has_groups(r):
                        continue
                    if p == 0 and r % PER_BLK < BI:
                        pe.wait_ge(gu_cast, B * GU_UNITS + (it + 1) * 4)
                    if p >= RING:
                        evac_wait(pe, s, p - RING)
                    elif r >= 1:
                        evac_wait(pe, s - 1, n + p - RING)
                    w = wgu[:, par, it, m, k * P:(k + 1) * P]
                    pe.matmul(bank(p % RING), w, xT[:, c, k, 0, :], start=True, stop=False)
                    pe.matmul(bank(p % RING), w, xT[:, c, k, 1, :], start=False, stop=True)\
                        .then_inc(group_ps, 1)

            schedule(pe, slot)


def kernel(x, L0_tok_A, L0_tok_B, L0_attn_Wqk_w, L0_attn_Wqk_b, L0_attn_Wv_w, L0_attn_Wv_b, L0_attn_Wo_w,
           L0_attn_Wo_b, L0_ffn_gate_q, L0_ffn_gate_s, L0_ffn_up_q, L0_ffn_up_s, L0_ffn_down_q, L0_ffn_down_s):
    import numpy as np
    import concourse.bacc as bacc
    from concourse.bass_utils import run_bass_kernel_spmd

    def arr(a):
        return np.asarray(a)

    nb, seq = x.shape
    D = L0_tok_B.shape[0]
    HD = L0_attn_Wv_w.shape[0]
    wqk = arr(L0_attn_Wqk_w).reshape(HD, 2, D)
    bqk = arr(L0_attn_Wqk_b).reshape(HD, 2)
    wqkv = np.concatenate([wqk[:, 0], wqk[:, 1], arr(L0_attn_Wv_w)], 0).T
    bqkv = np.concatenate([bqk[:, 0], bqk[:, 1], arr(L0_attn_Wv_b)])[None, :]

    def up_tiles(w):
        i, d = w.shape
        return arr(w).reshape(i // P, P, d // P, P).transpose(0, 3, 2, 1).reshape(i // P, P, d)

    def up_scales(s):
        i, g = s.shape
        return arr(s).reshape(i // (2 * P), 2, P, g).transpose(0, 2, 1, 3)

    gu_s = np.stack([up_scales(L0_ffn_gate_s), up_scales(L0_ffn_up_s)], 3)
    arrays = {
        "ids": arr(x).reshape(-1, P).T,
        "A_T": arr(L0_tok_A).T,
        "B_T": arr(L0_tok_B).T,
        "wqkv_T": wqkv,
        "qkv_b": bqkv,
        "wo_T": arr(L0_attn_Wo_w).T,
        "wo_b": arr(L0_attn_Wo_b),
        "gu_q": np.stack([up_tiles(L0_ffn_gate_q), up_tiles(L0_ffn_up_q)], 1),
        "gu_s": gu_s.reshape(gu_s.shape[0], P, -1),
        "dn_q": arr(L0_ffn_down_q).T.reshape(-1, P, D),
        "dn_s": arr(L0_ffn_down_s).T,
    }
    arrays = {k: np.ascontiguousarray(v) for k, v in arrays.items()}
    nc = bacc.Bacc("TRN2", target_bir_lowering=False, num_devices=1)
    args = [nc.dram_tensor(k, v.shape, mybir.dt.from_np(v.dtype), kind="ExternalInput").ap()
            for k, v in arrays.items()]
    out = nc.dram_tensor("out", (nb * seq, D), F32, kind="ExternalOutput").ap()
    lm_tower_kernel(nc, *args, out)
    got = run_bass_kernel_spmd(nc, [arrays], core_ids=[0])
    return got.results[0]["out"].reshape(nb, seq, D)
```

```python
from contextlib import ExitStack

import concourse.bass as bass
from concourse import mybir

ALU = mybir.AluOpType
ACT = mybir.ActivationFunctionType
AX = mybir.AxisListType
F32 = mybir.dt.float32
F16 = mybir.dt.float16
BF16 = mybir.dt.bfloat16
I32 = mybir.dt.int32

P = 128


def lm_tower_kernel(nc, ids, A_T, B_T, wqkv_T, qkv_b, wo_T, wo_b, gu_q, gu_s, dn_q, dn_s, out):
    NT = ids.shape[1]
    R, D = B_T.shape
    HD = wo_T.shape[0]
    H = 8
    E = HD // H
    KD = D // P
    NB = 4
    TB = NT // NB
    S = TB * P
    IT = gu_q.shape[0]
    BI = 2
    NBLK = IT // BI
    HALF = D // 2
    EPS = 1e-5
    TERMS = 6
    KS = TERMS * E
    KX = KS + 3
    EXP_UP = 10.39
    XS = 1024.0

    ctx = ExitStack()
    with ctx:
        def sb(name, shape, dt):
            return ctx.enter_context(nc.sbuf_tensor(name, shape, dt))

        def sem(name):
            return ctx.enter_context(nc.semaphore(name))

        hres = sb("hres", [P, NT, D], F32)
        xT = sb("xT", [P, NB, KD, 2, S], F16)
        wreg = sb("wreg", [P, 2, 2, BI, 2, D], F16)
        wgu, wdn = wreg[:, 0], wreg[:, 1]
        zT = sb("zT", [P, 2, BI, 2, S], F16)
        gsc = sb("gsc", [P, 2, BI, 2, KD], F32)
        qst = sb("qst", [P, 2, HALF], I32)
        sst = sb("sst", [P, 2, HALF], F32)
        sums = sb("sums", [P, 11 * S], F32)
        accd = sums[:, 0:2 * BI * S].rearrange("p (a b c) -> p a b c", a=BI, b=2)
        acca = sums[:, 2 * BI * S:4 * BI * S].rearrange("p (a b c) -> p a b c", a=BI, b=2)
        tmpa = sums[:, 4 * BI * S:(4 * BI + 2) * S].rearrange("p (b c) -> p b c", b=2)
        tnh = sums[:, (4 * BI + 2) * S:(4 * BI + 3) * S]
        oT = sb("oT", [P, 2, P], F32)
        identf = sb("identf", [P, P], F32)
        identb = sb("identb", [P, P], BF16)
        ids_sb = sb("ids_sb", [P, NT], I32)
        low = sb("low", [P, NT, R], F32)
        lowx = sb("lowx", [P, NT, R], F32)
        lres = sb("lres", [P, NT, R], F32)
        lpart = sb("lpart", [P, 2, NT, R], BF16)
        yl = sb("yl", [P, NT, R], F32)
        st1 = sb("st1", [P, TB, 2, 6], F32)
        mv1 = sb("mv1", [P, TB, 2], F32)
        rs1 = sb("rs1", [P, NT], F32)
        rs2 = sb("rs2", [P, TB], F32)
        nmean2 = sb("nmean2", [P, TB], F32)
        nmr2 = sb("nmr2", [P, TB], F32)
        mhalf = sb("mhalf", [P, NT], F32)
        nmax = sb("nmax", [P, TB], F32)
        nres = sb("nres", [P, TB], F32)
        nparts = sb("nparts", [P, 2, 3, TB], BF16)
        osum = sb("osum", [P, TB, E], F32)
        rden = sb("rden", [P, TB], F32)
        bmean = sb("bmean", [R, 1], F32)
        Bc = sb("Bc", [P, KD, R], F32)
        smax = sb("smax", [P, 4], F32)
        sall = sb("sall", [P, 4], F32)
        sexp = sb("sexp", [P, 8], I32)
        spow = sb("spow", [P, 8], I32)

        flat = wreg[:, :, :, :, :, :].rearrange("p w q a b c -> p (w q a b c)").bitcast(F32)
        wqkv = flat[:, 0:KD * 3 * HD].rearrange("p (k n) -> p k n", k=KD)
        BT = flat[0:R, 3072:4096]
        BcT = flat[0:R, 4096:5120]
        Bs = hres[:, NT - 1, 0:D // 2].bitcast(BF16)
        MC = 3 * HD + R
        Ms = flat[:, 6656:6656 + MC // 2].bitcast(BF16)
        lowTs = flat[:, 6912:7936].bitcast(BF16)
        part = flat[:, 0:1152].bitcast(BF16).rearrange("p (n j c) -> p n j c", n=2, j=3)
        res1 = flat[:, 1152:1920].rearrange("p (n c) -> p n c", n=2)
        stk = flat[:, 1920:1920 + 2 * H * KX].bitcast(BF16).rearrange("p (n x h c) -> p n x h c", n=2, x=2, h=H)
        qstack, kstack = stk[:, :, 0], stk[:, :, 1]
        ex32 = flat[:, 0:4096].rearrange("p (n k s) -> p n k s", n=2, k=TB)
        exhi = flat[:, 4096:6144].bitcast(F16).rearrange("p (n k s) -> p n k s", n=2, k=TB)
        exlo = flat[:, 6144:8192].bitcast(F16).rearrange("p (n k s) -> p n k s", n=2, k=TB)
        zflat = zT[:, :, :, :, :].rearrange("p q a b c -> p (q a b c)").bitcast(F32)
        woT = zflat[:, 0:D]
        lowTs0 = zflat[:, D:2 * D].bitcast(BF16)
        lstack = hres[:, NT - 2, 0:NT * KX // 2].bitcast(BF16).rearrange("p (n c) -> p n c", n=NT)
        VC = 3 * E + 1
        vend = TB * NB * H * VC // 2
        vparts = sums[:, 0:vend].bitcast(BF16).rearrange("p (t b h c) -> p t b h c", t=TB, b=NB, h=H)
        o_sb = sums[:, vend:vend + NT * HD].rearrange("p (t b c) -> p t b c", t=TB, b=NB)
        o_cur = sums[:, vend + NT * HD:vend + (NT + 2) * HD].rearrange("p (n c) -> p n c", n=2)
        xs = sums[:, 0:2 * D].rearrange("p (n c) -> p n c", n=2)
        vheads = vparts.rearrange("p t b h c -> p t (b h) c")
        xflat = xT[:, :, :, :, :].rearrange("p a b c d -> p (a b c d)").bitcast(BF16)
        qT = xflat[:, 0:NB * H * S].rearrange("p (u s) -> p u s", s=S)
        kT = xflat[:, NB * H * S:2 * NB * H * S].rearrange("p (u s) -> p u s", s=S)
        brow = hres[0:1, NT - 8, 0:2 * MC].rearrange("p (j c) -> p j c", j=2)
        bparts = hres[0:1, NT - 9, :].bitcast(BF16)[:, 0:3 * MC].rearrange("p (j c) -> p j c", j=3)
        bo = hres[0:1, 0:2, :]
        boparts = hres[0:1, NT - 11:NT - 9, :].rearrange("p a c -> p (a c)").bitcast(BF16)[:, 0:3 * D]\
            .rearrange("p (j c) -> p j c", j=3)
        Bres = hres[0:R, NT - 4, :]
        Bparts = hres[0:R, NT - 6:NT - 4, :].rearrange("p a c -> p (a c)").bitcast(BF16)[:, 0:3 * D]\
            .rearrange("p (j c) -> p j c", j=3)
        Mf = hres[0:R, NT - 13, 0:MC]
        Mres = hres[0:R, NT - 13, MC:2 * MC]
        Mparts = hres[0:R, NT - 7, :].bitcast(BF16)[:, 0:3 * MC].rearrange("p (j c) -> p j c", j=3)
        gs_ld = hres[:, NT - 3, 0:NBLK * BI * 2 * KD]
        ds_ld = hres[0:IT, NT - 14, :]

        banks = ctx.enter_context(nc.psum_tensor("banks", [P, 8, 512], F32))

        def bank(i, n=1):
            return banks[:, i, :] if n == 1 else banks[:, i:i + n, :]

        def bankb(i):
            return banks[:, i, :].bitcast(BF16)

        ids_in = sem("ids_in")
        BT_in = sem("BT_in")
        bias_in = sem("bias_in")
        wqkv_in = sem("wqkv_in")
        wo_in = sem("wo_in")
        bo_in = sem("bo_in")
        sall_in = sem("sall_in")
        gsc_in = [sem("gsc_in0"), sem("gsc_in1")]
        low_in = sem("low_in")
        ident_step = sem("ident_step")
        ones_set = sem("ones_set")
        smax_made = sem("smax_made")
        sall_made = sem("sall_made")
        spow_step = sem("spow_step")
        Bc_step = sem("Bc_step")
        BcT_ps = sem("BcT_ps")
        boparts_made = sem("boparts_made")
        Bc_made = sem("Bc_made")
        M_ps = sem("M_ps")
        chain = sem("chain")
        Bs_in = sem("Bs_in")
        Ms_in = sem("Ms_in")
        lstack_made = sem("lstack_made")
        lstackT_ps = sem("lstackT_ps")
        lowTs_made = sem("lowTs_made")
        y_ps = sem("y_ps")
        dve_step = sem("dve_step")
        waited = sem("waited")
        var1_made = sem("var1_made")
        rstd1_made = sem("rstd1_made")
        var2_made = sem("var2_made")
        rstd2_made = sem("rstd2_made")
        qkv_ps = sem("qkv_ps")
        part1_made = sem("part1_made")
        res1_made = sem("res1_made")
        part2_made = sem("part2_made")
        part3_made = sem("part3_made")
        v_made = sem("v_made")
        stacks_made = sem("stacks_made")
        stackT_ps = sem("stackT_ps")
        qT_made = sem("qT_made")
        kT_made = sem("kT_made")
        score_ps = sem("score_ps")
        max_made = sem("max_made")
        nparts_made = sem("nparts_made")
        nres_made = sem("nres_made")
        maxrow_ps = sem("maxrow_ps")
        maxrow_made = sem("maxrow_made")
        scoreT_ps = sem("scoreT_ps")
        exhi_made = sem("exhi_made")
        exlo_dve = sem("exlo_dve")
        exlo_pool = sem("exlo_pool")
        pv_ps = sem("pv_ps")
        norm_step = sem("norm_step")
        o_made = sem("o_made")
        ocur_made = sem("ocur_made")
        oT_ps = sem("oT_ps")
        oT_made = sem("oT_made")
        wo_ps = sem("wo_ps")
        h_made = sem("h_made")
        st2_made = sem("st2_made")
        shift2_made = sem("shift2_made")
        xs_made = sem("xs_made")
        xsT_ps = sem("xsT_ps")
        xhi_made = sem("xhi_made")
        xlo_made = sem("xlo_made")
        q_in = [sem("q_in0"), sem("q_in1")]
        s_in = [sem("s_in0"), sem("s_in1")]
        w_made = sem("w_made")
        whi_made = sem("whi_made")
        wlo_made = sem("wlo_made")
        gu_cast = sem("gu_cast")
        group_ps = sem("group_ps")
        act_evac = sem("act_evac")
        dve_evac = sem("dve_evac")
        pool_added = sem("pool_added")
        merged = sem("merged")
        tanh_made = sem("tanh_made")
        sg_made = sem("sg_made")
        zf_made = sem("zf_made")
        zhi_made = sem("zhi_made")
        zlo_made = sem("zlo_made")
        down_ps = sem("down_ps")
        down_added = sem("down_added")
        out_done = sem("out_done")

        def tiles(eng, slot, head, lag):
            turns = (NT - head) // TB
            for s in range(head):
                slot(s, s, 0)
            with eng.Fori(0, turns) as i:
                for r in range(head, head + TB):
                    slot(i * TB + r, r, i)
            for s in range(head + turns * TB, NT + lag):
                slot(s, s, 0)

        def tile_live(r, lag):
            return lag <= r < NT + lag

        NU = NB * H

        def heads(eng, slot):
            for s in range(4):
                slot(s, s, 0)
            with eng.Fori(0, (NU - 4) // 2) as i:
                for r in (4, 5):
                    slot(i * 2 + r, r, i)
            for s in range(NU, NU + 4):
                slot(s, s, 0)

        def live(r, lag):
            return lag <= r < NU + lag

        OWNER = "DADDADDADDADADAD"
        ND, NA = OWNER.count("D"), OWNER.count("A")
        GROUPS = []
        for p_, o_ in enumerate(OWNER):
            i_ = OWNER[:p_].count(o_)
            GROUPS.append((o_, i_, i_ % 2, i_ // 2 + (0 if o_ == "D" else ND // 2)))
        RING = 4
        LAG = BI + 1
        PER_BLK = NB * BI
        BODY = 2 * PER_BLK
        SLOTS = NBLK * PER_BLK
        TURNS = SLOTS // BODY - 1
        GU_UNITS = BI * 2 * 2
        DN_UNITS = BI * 2
        UNITS = GU_UNITS + DN_UNITS

        def evac_wait(eng, s, p):
            o, i, _, _ = GROUPS[p]
            eng.wait_ge(dve_evac if o == "D" else act_evac, s * (ND if o == "D" else NA) + i + 1)

        def schedule(eng, slot):
            for s in range(LAG + 1):
                slot(s, s, s // PER_BLK)
            with eng.Fori(0, TURNS) as i:
                for r in range(LAG + 1, LAG + 1 + BODY):
                    slot(i * BODY + r, r, i * 2 + r // PER_BLK)
            for s in range(TURNS * BODY + LAG + 1, SLOTS + LAG + 1):
                slot(s, s, s // PER_BLK)

        def gsc_loads(s, r, B):
            if isinstance(s, int):
                return 16 * (B // 2 + 1)
            return (s - r) // BODY * 16 + 16 * (r // BODY + 1)

        def has_groups(r):
            return r < SLOTS

        def has_z(r):
            return 1 <= r <= SLOTS

        def prefetch(r):
            q = r % PER_BLK
            if r >= SLOTS - PER_BLK:
                return [], []
            return ([2 * q, 2 * q + 1], []) if 2 * q < GU_UNITS else ([], [q - GU_UNITS // 2])

        def first_down_units(r):
            return [r - NT] if 0 <= r - NT < DN_UNITS else []

        def gu_unit(par, k):
            return wgu[:, par, k // 4, k // 2 % 2, (k % 2) * HALF:(k % 2 + 1) * HALF]

        def dn_unit(par, d):
            return wdn[:, par, d // 2, :, (d % 2) * HALF:(d % 2 + 1) * HALF]

        block = ctx.enter_context(nc.Block())

        def stand(eng):
            eng.sem_inc(waited, 1)

        @block.sync
        def _(sp):
            sp.dma_start(ids_sb[:, :], ids).then_inc(ids_in, 16)
            sp.dma_start(BT, B_T).then_inc(BT_in, 16)
            sp.dma_start(wqkv, wqkv_T.rearrange("(k p) n -> p k n", p=P)).then_inc(wqkv_in, 16)
            sp.dma_start(brow[:, 0, 0:3 * HD], qkv_b).then_inc(bias_in, 16)
            sp.dma_start(gs_ld.rearrange("p (b c) -> p b c", b=NBLK), gu_s.rearrange("b p c -> p b c"))\
                .then_inc(sall_in, 16)
            sp.dma_start(ds_ld, dn_s).then_inc(sall_in, 16)
            sp.dma_start(bo[:, 0, :], wo_b.partition_broadcast(1)).then_inc(bo_in, 16)
            sp.dma_start(woT, wo_T).then_inc(wo_in, 16)

            sp.wait_ge(chain, 4)
            for g, j in enumerate((0, 1, 2, 0, 1, 0)):
                sp.dma_start(Bs[g * R:(g + 1) * R, :], Bparts[:, j, :]).then_inc(Bs_in, 16)
            sp.wait_ge(chain, 14)
            for g, j in enumerate((0, 1, 2, 0, 1, 0)):
                sp.dma_start(Ms[g * R:(g + 1) * R, :], Mparts[:, j, :]).then_inc(Ms_in, 16)
            for j in range(3):
                sp.dma_start(Ms[KS + j:KS + j + 1, :], bparts[:, j, :]).then_inc(Ms_in, 16)
            sp.wait_ge(boparts_made, 1)
            for j in range(3):
                sp.dma_start(Bs[KS + j:KS + j + 1, :], boparts[:, j, :]).then_inc(Bs_in, 16)

            def load_block(B):
                first = isinstance(B, int) and B == 0
                for k in range(UNITS):
                    if not first or k >= 2:
                        if 2 <= k < 2 + GU_UNITS:
                            sp.wait_ge(gu_cast, B * GU_UNITS + k - 1)
                            stand(sp)
                        else:
                            sp.wait_ge(w_made, B * DN_UNITS + k - 1 - (GU_UNITS if k >= 2 else 0))
                            stand(sp)
                    if k < GU_UNITS:
                        src = gu_q[B * BI + k // 4, k // 2 % 2]
                    else:
                        d = k - GU_UNITS
                        src = dn_q[B * BI + d // 2]
                    sp.dma_start(qst[:, k % 2, :], src[:, (k % 2) * HALF:(k % 2 + 1) * HALF])\
                        .then_inc(q_in[k % 2], 16)
                    if k >= GU_UNITS:
                        if not first or d >= 2:
                            sp.wait_ge(wlo_made, B * DN_UNITS + d - 1)
                            stand(sp)
                        sp.dma_start(sst[:, d % 2, :], dn_s[B * BI + d // 2, (d % 2) * HALF:(d % 2 + 1) * HALF]
                                     .partition_broadcast(P)).then_inc(s_in[d % 2], 16)

            def load_scales(B, par):
                sp.dma_start(gsc[:, par, :, :, :].rearrange("p a b c -> p (a b c)"), gu_s[B])\
                    .then_inc(gsc_in[par], 16)

            load_scales(0, 0)
            load_scales(1, 1)
            load_block(0)
            with sp.Fori(0, NBLK // 2 - 1) as i:
                for par in range(2):
                    load_block(i * 2 + 1 + par)
                    sp.wait_ge(dve_evac, (i * 2 + par + 1) * (PER_BLK * ND))
                    stand(sp)
                    sp.wait_ge(act_evac, (i * 2 + par + 1) * (PER_BLK * NA))
                    stand(sp)
                    load_scales(i * 2 + par + 2, par)
            load_block(NBLK - 1)

            for t in range(NT):
                sp.wait_ge(down_added, 2 + (NBLK - 1) * NT + t + 1)
                sp.dma_start(out[t * P:(t + 1) * P, :], hres[:, t, :]).then_inc(out_done, 16)
            sp.wait_ge(out_done, 16 * NT)

        @block.gpsimd
        def _(pool):
            pool.memset(identf[:, :], 0.0).then_inc(ident_step, 1)
            pool.memset(identb[:, :], 0.0).then_inc(ident_step, 1)
            pool.wait_ge(ident_step, 2)
            for m in (identf, identb):
                pool.affine_select(out=m[:, :], in_=m[:, :], compare_op=ALU.not_equal, fill=1.0, base=0,
                                   pattern=[[-1, P]], channel_multiplier=1).then_inc(ident_step, 1)
            pool.wait_ge(ids_in, 16)
            for t in range(NT):
                pool.indirect_dma_start(out=low[:, t, :], out_offset=None, in_=A_T,
                                        in_offset=bass.IndirectOffsetOnAxis(ap=ids_sb[:, t:t + 1], axis=0))\
                    .then_inc(low_in, 16)
            pool.memset(mhalf[:, :], -0.5).then_inc(ones_set, 1)
            pool.memset(vparts[:, :, :, :, 3 * E:VC].rearrange("p t b h c -> p (t b h) c"), 1.0)\
                .then_inc(ones_set, 1)
            pool.wait_ge(smax_made, 2)
            pool.partition_all_reduce(sall[:, 0:3], smax[:, 0:3], P, bass.bass_isa.ReduceOp.max)\
                .then_inc(sall_made, 1)
            pool.wait_ge(ones_set, 3)
            pool.wait_ge(var1_made, 1)
            pool.tensor_tensor(rs1[:, :], rs1[:, :], mhalf[:, :], ALU.pow).then_inc(rstd1_made, 1)

            def qkv_slot(s, r, i):
                if tile_live(r, 1):
                    p, t, b = (r - 1) % 2, (r - 1) % TB, i + (r - 1) // TB
                    pool.wait_ge(part2_made, s)
                    pool.tensor_tensor(part[:, p, 2, 0:2 * HD], res1[:, p, 0:2 * HD], part[:, p, 1, 0:2 * HD],
                                       ALU.subtract).then_inc(part3_made, 1)
                    pool.tensor_tensor(vparts[:, t, b, :, 2 * E:3 * E],
                                       res1[:, p, 2 * HD:3 * HD].rearrange("p (h e) -> p h e", h=H),
                                       part[:, p, 1, 2 * HD:3 * HD].rearrange("p (h e) -> p h e", h=H),
                                       ALU.subtract).then_inc(v_made, 1)

            tiles(pool, qkv_slot, 4, 3)

            def head_slot(s, r, i):
                if live(r, 2):
                    if r >= 4:
                        pool.wait_ge(pv_ps, s - 3)
                    pool.wait_ge(exhi_made, s * 2 - 3)
                    pool.tensor_tensor(exlo[:, r % 2, 1, :], ex32[:, r % 2, 1, :], exhi[:, r % 2, 1, :],
                                       ALU.subtract)
                    pool.wait_ge(exhi_made, s * 2 - 2)
                    pool.tensor_tensor(exlo[:, r % 2, 2:4, :], ex32[:, r % 2, 2:4, :], exhi[:, r % 2, 2:4, :],
                                       ALU.subtract).then_inc(exlo_pool, 1)

            heads(pool, head_slot)

            def split_lo(B, par, d):
                pool.wait_ge(whi_made, B * DN_UNITS + d + 1)
                w = dn_unit(par, d)
                pool.tensor_tensor(w[:, 1, :], sst[:, d % 2, :], w[:, 0, :], ALU.subtract)\
                    .then_inc(wlo_made, 1)

            def slot(s, r, B):
                it, pit, pz = r % BI, (r - 1) % BI, (r - 1) // BI % 2

                def add(i):
                    m = i % 2
                    pool.wait_ge(act_evac, s * NA + i + 1)
                    if i >= 4:
                        pool.wait_ge(pool_added, s * (NA - 2) + i - 3)
                    pool.tensor_tensor(acca[:, it, m, :], acca[:, it, m, :], tmpa[:, m, :], ALU.add)\
                        .then_inc(pool_added, 1)

                if has_z(r):
                    for m in range(2):
                        pool.wait_ge(dve_evac, (s - 1) * ND + ND - 1 + m)
                        pool.wait_ge(pool_added, (s - 1) * (NA - 2) + NA - 3 + m)
                        pool.tensor_tensor(accd[:, pit, m, :], accd[:, pit, m, :], acca[:, pit, m, :],
                                           ALU.add).then_inc(merged, 1)
                if has_groups(r):
                    for i in range(2, 4):
                        add(i)
                if has_z(r):
                    pool.wait_ge(zhi_made, s)
                    pool.tensor_tensor(zT[:, pz, pit, 1, :], accd[:, pit, 1, :], zT[:, pz, pit, 0, :],
                                       ALU.subtract).then_inc(zlo_made, 1)
                if has_groups(r):
                    for i in range(4, NA):
                        add(i)
                for d in prefetch(r)[1]:
                    split_lo(B + 1, (r // PER_BLK + 1) % 2, d)

            def norm_slot(s, r, i):
                if tile_live(r, 2):
                    t = (r - 2) % TB
                    pool.wait_ge(var2_made, s - 1)
                    pool.tensor_tensor(rs2[:, t:t + 1], rs2[:, t:t + 1], mhalf[:, 0:1], ALU.pow)\
                        .then_inc(rstd2_made, 1)
                    pool.wait_ge(rstd2_made, s - 1)
                    pool.tensor_tensor(nmr2[:, t:t + 1], nmean2[:, t:t + 1], rs2[:, t:t + 1], ALU.mult)\
                        .then_inc(shift2_made, 1)
                for d in first_down_units(r):
                    split_lo(0, 0, d)

            tiles(pool, norm_slot, 5, 4)
            schedule(pool, slot)

        @block.scalar
        def _(act):
            act.wait_ge(BcT_ps, 1)
            act.activation(Bc[:, :, :].rearrange("p k r -> p (k r)"), bank(6)[:, 0:KD * R], ACT.Copy)\
                .then_inc(Bc_made, 1)
            for c, dst in enumerate((lowTs0, lowTs)):
                for a in range(2):
                    act.wait_ge(lstackT_ps, 2 * c + a + 1)
                    act.activation(dst[0:KX, a * 1024:(a + 1) * 1024], bankb(4 + a)[0:KX, :], ACT.Copy)\
                        .then_inc(lowTs_made, 1)

            def qkv_slot(s, r, i):
                p = r % 2
                if tile_live(r, 0):
                    if r >= 2:
                        act.wait_ge(stacks_made, s - 1)
                        act.wait_ge(v_made, s - 1)
                    act.wait_ge(qkv_ps, s + 1)
                    act.activation(part[:, p, 0, :], bank(p)[:, 0:3 * HD], ACT.Copy).then_inc(part1_made, 1)
                if tile_live(r, 3):
                    t, b = (r - 3) % TB, i + (r - 3) // TB
                    act.wait_ge(stackT_ps, s - 2)
                    act.activation(kT[0:KX, bass.ds(b * H, H), t * P:(t + 1) * P] if not isinstance(s, int) else
                                   kT[0:KX, b * H:(b + 1) * H, t * P:(t + 1) * P],
                                   bankb(5 + 2 * (1 - p))[0:KX, :].rearrange("p (h s) -> p h s", h=H), ACT.Copy)\
                        .then_inc(kT_made, 1)
                if tile_live(r, 0):
                    act.wait_ge(res1_made, s + 1)
                    act.activation(part[:, p, 1, :], res1[:, p, :], ACT.Copy).then_inc(part2_made, 1)

            tiles(act, qkv_slot, 4, 3)

            def head_slot(s, r, i):
                if live(r, 2) and r >= 4:
                    act.wait_ge(exlo_dve, s - 3)
                    act.wait_ge(exlo_pool, s - 3)
                    act.wait_ge(pv_ps, s - 3)
                for j in range(2):
                    if live(r, 2):
                        act.wait_ge(scoreT_ps, s * 2 - 3 + j)
                        act.activation(ex32[:, r % 2, 2 * j:2 * j + 2, :], bank(2 + 2 * j, 2), ACT.Exp)
                        act.activation(exhi[:, r % 2, 2 * j:2 * j + 2, :], bank(2 + 2 * j, 2), ACT.Exp)\
                            .then_inc(exhi_made, 1)
                    if j == 0 and live(r, 1):
                        act.wait_ge(maxrow_ps, s)
                        act.activation(qT[KS:KX, s - 1, :] if isinstance(s, int) else
                                       qT[KS:KX, bass.ds(s - 1, 1), :].rearrange("p a s -> p (a s)"),
                                       bank(6)[KS:KX, :], ACT.Copy).then_inc(maxrow_made, 1)

            heads(act, head_slot)

            def cast_gu(B, par, k):
                act.wait_ge(q_in[k % 2], B * (8 * UNITS) + (k // 2 + 1) * 16)
                act.activation(gu_unit(par, k), qst[:, k % 2, :], ACT.Copy).then_inc(gu_cast, 1)

            def split_hi(B, par, d):
                act.wait_ge(w_made, B * DN_UNITS + d + 1)
                act.activation(dn_unit(par, d)[:, 0, :], sst[:, d % 2, :], ACT.Copy).then_inc(whi_made, 1)

            def slot(s, r, B):
                it, pit, pz, par = r % BI, (r - 1) % BI, (r - 1) // BI % 2, r // PER_BLK % 2
                for p, (o, i, m, k) in enumerate(GROUPS):
                    if o == "D" or not has_groups(r):
                        continue
                    if i == 0 and r % PER_BLK == 0:
                        act.wait_ge(gsc_in[par], gsc_loads(s, r, B))
                    act.wait_ge(group_ps, s * (ND + NA) + p + 1)
                    if i < 2:
                        dst = acca[:, it, m, :]
                        if r >= BI:
                            act.wait_ge(merged, s * 2 - 3 + m)
                    else:
                        dst = tmpa[:, m, :]
                        if r >= 1 or i >= 4:
                            act.wait_ge(pool_added, s * (NA - 2) + i - 3)
                    act.activation(dst, bank(p % RING), ACT.Copy, scale=gsc[:, par, it, m, k:k + 1])\
                        .then_inc(act_evac, 1)
                    if i == 1:
                        tanh(s, r)
                    if i == 3:
                        z_hi(s, r)
                if not has_groups(r):
                    tanh(s, r)
                    z_hi(s, r)
                for k in prefetch(r)[0]:
                    cast_gu(B + 1, 1 - par, k)
                for d in prefetch(r)[1]:
                    split_hi(B + 1, 1 - par, d)

            def tanh(s, r):
                if has_z(r):
                    act.wait_ge(merged, s * 2 - 1)
                    if r >= 2:
                        act.wait_ge(zf_made, s - 1)
                    act.activation(tnh[:, :], accd[:, (r - 1) % BI, 0, :], ACT.Tanh, scale=0.5 / XS)\
                        .then_inc(tanh_made, 1)

            def z_hi(s, r):
                if has_z(r):
                    act.wait_ge(zf_made, s)
                    act.activation(zT[:, (r - 1) // BI % 2, (r - 1) % BI, 0, :], accd[:, (r - 1) % BI, 1, :],
                                   ACT.Copy).then_inc(zhi_made, 1)

            def norm_slot(s, r, i):
                if tile_live(r, 0):
                    if r >= 2:
                        act.wait_ge(wo_ps, s - 1)
                    act.wait_ge(oT_ps, s + 1)
                    act.activation(oT[:, r % 2, :], bank(r % 2)[:, 0:HD], ACT.Copy).then_inc(oT_made, 1)
                if tile_live(r, 3):
                    t, b = (r - 3) % TB, i + (r - 3) // TB
                    for j in range(2):
                        act.wait_ge(xsT_ps, s * 2 - 5 + j)
                        act.activation(xT[:, b, 4 * j:4 * j + 4, 0, t * P:(t + 1) * P],
                                       bank(6 + j).rearrange("p (k s) -> p k s", k=4),
                                       ACT.Copy).then_inc(xhi_made, 1)
                if tile_live(r, 1):
                    act.wait_ge(st2_made, s)
                    stand(act)
                    act.activation(hres[:, i * TB + (r - 1), :].rearrange("p (a c) -> p a c", a=2),
                                   bank(2 + 2 * ((r - 1) % 2), 2), ACT.Copy).then_inc(h_made, 1)
                if tile_live(r, 2):
                    t, n = (r - 2) % TB, i * TB + (r - 2)
                    if r >= 4:
                        act.wait_ge(xsT_ps, s * 2 - 6)
                    act.wait_ge(shift2_made, s - 1)
                    act.wait_ge(h_made, s - 1)
                    stand(act)
                    act.activation(xs[:, r % 2, :], hres[:, n, :], ACT.Identity, scale=rs2[:, t:t + 1],
                                   bias=nmr2[:, t:t + 1]).then_inc(xs_made, 1)
                if 2 * r < GU_UNITS:
                    for k in (2 * r, 2 * r + 1):
                        cast_gu(0, 0, k)
                for d in first_down_units(r):
                    split_hi(0, 0, d)

            act.wait_ge(pv_ps, NU)
            act.wait_ge(exlo_pool, NU)
            tiles(act, norm_slot, 5, 4)
            schedule(act, slot)

        @block.vector
        def _(dve):
            done = [0]

            def link(ins):
                done[0] += 1
                ins.then_inc(chain, 1)
                dve.wait_ge(chain, done[0])

            def fill(stack, parts):
                last = None
                for j, (a, c) in enumerate(((0, 3), (3, 5), (5, 6))):
                    last = dve.tensor_copy(stack[:, :, a:c, :],
                                           parts(j).unsqueeze(2).broadcast_to([P, stack.shape[1], c - a, E]))
                return last

            dve.wait_ge(BT_in, 16)
            dve.tensor_reduce(bmean[:, :], BT, AX.X, ALU.add).then_inc(Bc_step, 1)
            dve.wait_ge(Bc_step, 1)
            dve.tensor_scalar(bmean[:, :], bmean[:, :], 1.0 / D, None, ALU.mult).then_inc(Bc_step, 1)
            dve.wait_ge(Bc_step, 2)
            dve.tensor_scalar(BcT, BT, bmean[:, 0:1], None, ALU.subtract).then_inc(Bc_step, 1)

            link(dve.tensor_scalar(Bparts[:, 0, :], BT, 2.0, None, ALU.mult))
            link(dve.scalar_tensor_tensor(out=Bres, in0=BT, scalar=2.0, in1=Bparts[:, 0, :], op0=ALU.mult,
                                          op1=ALU.subtract))
            link(dve.tensor_copy(Bparts[:, 1, :], Bres))
            link(dve.tensor_tensor(Bparts[:, 2, :], Bres, Bparts[:, 1, :], ALU.subtract))

            dve.wait_ge(bias_in, 16)
            link(dve.memset(brow[:, 0, 3 * HD:MC], 0.0))
            link(dve.tensor_copy(bparts[:, 0, :], brow[:, 0, :]))
            link(dve.tensor_tensor(brow[:, 1, :], brow[:, 0, :], bparts[:, 0, :], ALU.subtract))
            link(dve.tensor_copy(bparts[:, 1, :], brow[:, 1, :]))
            link(dve.tensor_tensor(bparts[:, 2, :], brow[:, 1, :], bparts[:, 1, :], ALU.subtract))

            dve.wait_ge(sall_in, 32)
            dve.memset(smax[:, :], 0.0).then_inc(smax_made, 1)
            dve.wait_ge(smax_made, 1)
            gs_v = gs_ld.rearrange("p (t m k) -> p m t k", t=IT, m=2)
            for m in range(2):
                dve.tensor_reduce(smax[:, m:m + 1], gs_v[:, m], AX.XY, ALU.max, apply_absolute_value=True)
            dve.tensor_reduce(smax[0:IT, 2:3], ds_ld, AX.X, ALU.max, apply_absolute_value=True)\
                .then_inc(smax_made, 1)

            dve.wait_ge(M_ps, 1)
            link(dve.tensor_copy(Mf, bank(7)[0:R, 0:MC]))
            link(dve.tensor_copy(Mparts[:, 0, :], Mf))
            link(dve.tensor_tensor(Mres, Mf, Mparts[:, 0, :], ALU.subtract))
            link(dve.tensor_copy(Mparts[:, 1, :], Mres))
            link(dve.tensor_tensor(Mparts[:, 2, :], Mres, Mparts[:, 1, :], ALU.subtract))
            for p in range(2):
                dve.memset(kstack[:, p, :, KS:KX], 1.0)
            dve.memset(lstack[:, :, KS:KX], 1.0).then_inc(ones_set, 1)

            def low_stack(src):
                lv = lstack[:, :, 0:KS].rearrange("p n (r e) -> p n r e", r=TERMS)
                link(dve.tensor_copy(lpart[:, 0], src))
                link(dve.tensor_tensor(lres[:, :, :], src, lpart[:, 0], ALU.subtract))
                link(dve.tensor_copy(lpart[:, 1], lres[:, :, :]))
                for a, c, j in ((0, 3, 0), (3, 5, 1)):
                    dve.tensor_copy(lv[:, :, a:c, :], lpart[:, j].unsqueeze(2).broadcast_to([P, NT, c - a, R]))
                dve.tensor_tensor(lv[:, :, 5, :], lres[:, :, :], lpart[:, 1], ALU.subtract)\
                    .then_inc(lstack_made, 1)

            dve.wait_ge(low_in, 16 * NT)
            low_stack(low[:, :, :])

            dve.wait_ge(sall_made, 1)
            dve.tensor_single_scalar(sexp[:, 0:3], sall[:, 0:3].bitcast(I32), 23, ALU.logical_shift_right)\
                .then_inc(spow_step, 1)
            dve.wait_ge(spow_step, 1)
            dve.tensor_scalar(sexp[:, 0:3], sexp[:, 0:3], 64, None, ALU.max).then_inc(spow_step, 1)
            dve.wait_ge(spow_step, 2)
            dve.tensor_scalar(sexp[:, 4:5], sexp[:, 2:3], -1, 265, ALU.mult, ALU.add).then_inc(spow_step, 1)
            dve.tensor_tensor(sexp[:, 6:7], sexp[:, 0:1], sexp[:, 1:2], ALU.add).then_inc(spow_step, 1)
            dve.wait_ge(spow_step, 4)
            dve.tensor_tensor(sexp[:, 7:8], sexp[:, 6:7], sexp[:, 2:3], ALU.add).then_inc(spow_step, 1)
            dve.tensor_scalar(sexp[:, 5:6], sexp[:, 6:7], -1, 347, ALU.mult, ALU.add).then_inc(spow_step, 1)
            dve.wait_ge(spow_step, 6)
            dve.tensor_scalar(sexp[:, 7:8], sexp[:, 7:8], -252, 1, ALU.add, ALU.max).then_inc(spow_step, 1)
            dve.tensor_scalar(sexp[:, 5:6], sexp[:, 5:6], 1, 254, ALU.max, ALU.min).then_inc(spow_step, 1)
            dve.wait_ge(spow_step, 8)
            dve.tensor_scalar(sexp[:, 7:8], sexp[:, 7:8], 254, None, ALU.min).then_inc(spow_step, 1)
            dve.wait_ge(spow_step, 9)
            dve.tensor_single_scalar(spow[:, 4:8], sexp[:, 4:8], 23, ALU.logical_shift_left)\
                .then_inc(spow_step, 1)

            dve.wait_ge(y_ps, 1)
            link(dve.tensor_tensor(yl[:, :, :], bank(0)[:, 0:NT * R].rearrange("p (n r) -> p n r", n=NT),
                                   low[:, :, :], ALU.mult))
            link(dve.tensor_reduce(rs1[:, :], yl[:, :, :], AX.X, ALU.add))
            link(dve.tensor_scalar(rs1[:, :], rs1[:, :], 0.0, 4.0 / D, ALU.max, ALU.mult))
            dve.tensor_scalar(rs1[:, :], rs1[:, :], EPS, None, ALU.add).then_inc(var1_made, 1)

            dve.wait_ge(bo_in, 16)
            link(dve.tensor_copy(boparts[:, 0, :], bo[:, 0, :]))
            link(dve.tensor_tensor(bo[:, 1, :], bo[:, 0, :], boparts[:, 0, :], ALU.subtract))
            link(dve.tensor_copy(boparts[:, 1, :], bo[:, 1, :]))
            dve.tensor_tensor(boparts[:, 2, :], bo[:, 1, :], boparts[:, 1, :], ALU.subtract)\
                .then_inc(boparts_made, 1)

            dve.wait_ge(rstd1_made, 1)
            dve.wait_ge(lstackT_ps, 2)
            link(dve.scalar_tensor_tensor(out=lowx[:, :, :], in0=low[:, :, :], scalar=2.0,
                                          in1=rs1[:, :].unsqueeze(2).broadcast_to([P, NT, R]),
                                          op0=ALU.mult, op1=ALU.mult))
            low_stack(lowx[:, :, :])

            def qkv_slot(s, r, i):
                if tile_live(r, 0):
                    p = r % 2
                    if r >= 2:
                        dve.wait_ge(v_made, s - 1)
                    dve.wait_ge(part1_made, s + 1)
                    dve.tensor_tensor(res1[:, p, :], bank(p)[:, 0:3 * HD], part[:, p, 0, :],
                                      ALU.subtract).then_inc(res1_made, 1)
                if tile_live(r, 1):
                    p, t, b = (r - 1) % 2, (r - 1) % TB, i + (r - 1) // TB
                    dve.wait_ge(part3_made, s)
                    if r >= 3:
                        dve.wait_ge(stackT_ps, s - 2)
                    stand(dve)
                    qs = qstack[:, p, :, 0:KS].rearrange("p h (r e) -> p h r e", r=TERMS)
                    ks = kstack[:, p, :, 0:KS].rearrange("p h (r e) -> p h r e", r=TERMS)

                    def pt(j, x):
                        return part[:, p, j, x * HD:(x + 1) * HD].rearrange("p (h e) -> p h e", h=H)
                    fill(qs, lambda j: pt(j, 0))
                    dve.tensor_copy(ks[:, :, 0:6:3, :], pt(0, 1).unsqueeze(2).broadcast_to([P, H, 2, E]))
                    dve.tensor_copy(ks[:, :, 5, :], pt(0, 1))
                    dve.tensor_copy(ks[:, :, 1:5:3, :], pt(1, 1).unsqueeze(2).broadcast_to([P, H, 2, E]))
                    dve.tensor_copy(ks[:, :, 2, :], pt(2, 1))
                    dve.tensor_copy(vparts[:, t, b, :, 0:E], pt(0, 2))
                    dve.tensor_copy(vparts[:, t, b, :, E:2 * E], pt(1, 2)).then_inc(stacks_made, 1)
                if tile_live(r, 3):
                    t, b = (r - 3) % TB, i + (r - 3) // TB
                    dve.wait_ge(stackT_ps, s - 2)
                    dve.tensor_copy(qT[0:KS, bass.ds(b * H, H), t * P:(t + 1) * P] if not isinstance(s, int) else
                                    qT[0:KS, b * H:(b + 1) * H, t * P:(t + 1) * P],
                                    bankb(4 + 2 * ((r - 3) % 2))[0:KS, :].rearrange("p (h s) -> p h s", h=H))\
                        .then_inc(qT_made, 1)

            tiles(dve, qkv_slot, 4, 3)

            def head_slot(s, r, i):
                po = bank(7)[:, 0:TB * VC].rearrange("p (t c) -> p t c", t=TB)
                if live(r, 4):
                    dve.wait_ge(pv_ps, s - 3)
                    dve.tensor_scalar(rden[:, :], po[:, :, 3 * E], float(HD) ** 0.5, None, ALU.mult)\
                        .then_inc(norm_step, 1)
                    dve.tensor_reduce(osum[:, :, :], po[:, :, 0:3 * E].rearrange("p t (j e) -> p t e j", j=3),
                                      AX.X, ALU.add)
                    dve.wait_ge(norm_step, s * 2 - 7)
                    dve.reciprocal(rden[:, :], rden[:, :]).then_inc(norm_step, 1)
                for t in range(TB):
                    if live(r, 0):
                        dve.wait_ge(score_ps, s * TB + t + 1)
                        dve.reduce_max(nmax[:, t:t + 1], bank(t % 2), AX.X, negate=True).then_inc(max_made, 1)
                    if t == 0 and live(r, 4):
                        dve.wait_ge(norm_step, s * 2 - 6)
                        ov = o_sb.rearrange("p t b c -> p t (b c)")
                        dve.tensor_tensor(ov[:, :, bass.ds((s - 4) * E, E)], osum[:, :, :],
                                          rden[:, :].unsqueeze(2).broadcast_to([P, TB, E]), ALU.mult)\
                            .then_inc(o_made, 1)
                    if t == 2 and live(r, 2):
                        dve.wait_ge(exhi_made, s * 2 - 3)
                        if r >= 4:
                            dve.wait_ge(pv_ps, s - 3)
                        dve.tensor_tensor(exlo[:, r % 2, 0, :], ex32[:, r % 2, 0, :], exhi[:, r % 2, 0, :],
                                          ALU.subtract).then_inc(exlo_dve, 1)
                np_ = nparts[:, r % 2]
                if live(r, 0):
                    dve.wait_ge(max_made, s * TB + TB)
                    if r >= 2:
                        dve.wait_ge(maxrow_ps, s - 1)
                    dve.tensor_copy(np_[:, 0, :], nmax[:, :]).then_inc(nparts_made, 1)
                if live(r, 0):
                    dve.wait_ge(nparts_made, s * 3 + 1)
                    dve.tensor_tensor(nres[:, :], nmax[:, :], np_[:, 0, :], ALU.subtract).then_inc(nres_made, 1)
                    dve.tensor_tensor(np_[:, 1, :], nmax[:, :], np_[:, 0, :], ALU.subtract)\
                        .then_inc(nparts_made, 1)
                    dve.wait_ge(nres_made, s + 1)
                    dve.wait_ge(nparts_made, s * 3 + 2)
                    dve.scalar_tensor_tensor(out=np_[:, 2, :], in0=nres[:, :], scalar=EXP_UP, in1=np_[:, 1, :],
                                             op0=ALU.add, op1=ALU.subtract).then_inc(nparts_made, 1)

            heads(dve, head_slot)

            def norm_slot(s, r, i):
                def low_part(j):
                    if tile_live(r, 3):
                        t, b = (r - 3) % TB, i + (r - 3) // TB
                        dve.wait_ge(xhi_made, s * 2 - 5 + j)
                        xd = xT[:, b, 4 * j:4 * j + 4, :, t * P:(t + 1) * P]
                        dve.tensor_tensor(xd[:, :, 1, :], bank(6 + j)
                                          .rearrange("p (k s) -> p k s", k=4), xd[:, :, 0, :], ALU.subtract)\
                            .then_inc(xlo_made, 1)

                if tile_live(r, 0):
                    if r >= 2:
                        dve.wait_ge(oT_ps, s - 1)
                    dve.tensor_copy(o_cur[:, r % 2, :], o_sb[:, r % TB, i + r // TB, :]).then_inc(ocur_made, 1)
                t = (r - 1) % TB
                if tile_live(r, 1):
                    dve.wait_ge(wo_ps, s)
                    stand(dve)
                    for j in range(2):
                        x = dve.bn_stats(st1[:, t, j, :], bank(2 + 2 * ((r - 1) % 2) + j))
                    x.then_inc(st2_made, 1)
                low_part(0)
                if tile_live(r, 1):
                    dve.wait_ge(st2_made, s)
                    stand(dve)
                    dve.bn_aggr(mv1[:, t, :], st1[:, t, :, :].rearrange("p a b -> p (a b)")).then_inc(dve_step, 1)
                low_part(1)
                if tile_live(r, 1):
                    dve.wait_ge(dve_step, s)
                    dve.tensor_scalar(nmean2[:, t:t + 1], mv1[:, t, 0:1], -1.0, None, ALU.mult)
                    dve.tensor_scalar(rs2[:, t:t + 1], mv1[:, t, 1:2], XS ** -2, EPS * XS ** -2, ALU.mult, ALU.add)\
                        .then_inc(var2_made, 1)
                for d in first_down_units(r):
                    dequant(0, 0, d)

            def dequant(B, par, d):
                dve.wait_ge(q_in[d % 2], B * (8 * UNITS) + 8 * GU_UNITS + (d // 2 + 1) * 16)
                dve.wait_ge(s_in[d % 2], B * (8 * DN_UNITS) + (d // 2 + 1) * 16)
                dve.scalar_tensor_tensor(out=sst[:, d % 2, :], in0=qst[:, d % 2, :],
                                         scalar=spow[:, 4:5].bitcast(F32), in1=sst[:, d % 2, :],
                                         op0=ALU.mult, op1=ALU.mult).then_inc(w_made, 1)

            dve.wait_ge(o_made, NU)
            tiles(dve, norm_slot, 5, 4)

            dve.sem_inc(down_added, 2)

            def down_add(count, r):
                t = (r - LAG) // BI % NB * TB + (r - LAG) % BI * 2
                hv = hres[:, t + 1 if count[1] else t, :].rearrange("p (a c) -> p a c", a=2)
                dve.wait_ge(down_ps, count[0])
                dve.scalar_tensor_tensor(out=hv, in0=bank(4 + 2 * count[1], 2), scalar=spow[:, 7:8].bitcast(F32),
                                         in1=hv, op0=ALU.mult, op1=ALU.add).then_inc(down_added, 1)

            def slot(s, r, B):
                it, pit, par = r % BI, (r - 1) % BI, r // PER_BLK % 2

                def second_tile():
                    if LAG + 1 <= r <= SLOTS + LAG:
                        down_add(((s - LAG) * 2, 1), r - 1)

                def first_tile():
                    if LAG <= r < SLOTS + LAG:
                        down_add(((s - LAG) * 2 + 1, 0), r)

                def z():
                    if has_z(r):
                        dve.wait_ge(tanh_made, s)
                        dve.scalar_tensor_tensor(out=tnh[:, :], in0=tnh[:, :], scalar=1.0,
                                                 in1=accd[:, pit, 0, :], op0=ALU.add, op1=ALU.mult)\
                            .then_inc(sg_made, 1)
                        dve.wait_ge(sg_made, s)
                        dve.wait_ge(merged, s * 2)
                        dve.scalar_tensor_tensor(out=accd[:, pit, 1, :], in0=tnh[:, :],
                                                 scalar=spow[:, 5:6].bitcast(F32), in1=accd[:, pit, 1, :],
                                                 op0=ALU.mult, op1=ALU.mult).then_inc(zf_made, 1)

                if not has_groups(r):
                    second_tile()
                    z()
                    first_tile()
                    return
                for p, (o, i, m, k) in enumerate(GROUPS):
                    if o == "A":
                        continue
                    if i == 0 and r % PER_BLK == 0:
                        dve.wait_ge(gsc_in[par], gsc_loads(s, r, B))
                    acc, sc = accd[:, it, m, :], gsc[:, par, it, m, k:k + 1]
                    dve.wait_ge(group_ps, s * (ND + NA) + p + 1)
                    if i < 2:
                        if r >= BI:
                            dve.wait_ge(zlo_made, s - 1)
                        dve.tensor_scalar(acc, bank(p % RING), sc, None, ALU.mult).then_inc(dve_evac, 1)
                    else:
                        dve.wait_ge(dve_evac, s * ND + i - 1)
                        dve.scalar_tensor_tensor(out=acc, in0=bank(p % RING), scalar=sc, in1=acc,
                                                 op0=ALU.mult, op1=ALU.add).then_inc(dve_evac, 1)
                    if i == 1:
                        second_tile()
                    if i == 4:
                        z()
                    if i == 7:
                        first_tile()
                for d in prefetch(r)[1]:
                    dequant(B + 1, 1 - par, d)

            schedule(dve, slot)

        @block.tensor
        def _(pe):
            pe.wait_ge(ident_step, 4)
            pe.wait_ge(Bc_step, 3)
            for k in range(KD):
                i = pe.transpose(bank(6)[:, k * R:(k + 1) * R], BcT[:, k * P:(k + 1) * P], identf[0:R, 0:R])
            i.then_inc(BcT_ps, 1)
            pe.wait_ge(Bc_made, 1)
            pe.wait_ge(wqkv_in, 16)
            for k in range(KD):
                pe.matmul(bank(7)[0:R, 0:3 * HD], Bc[:, k, :], wqkv[:, k, :], start=(k == 0), stop=(k == KD - 1))
            for k in range(KD):
                i = pe.matmul(bank(7)[0:R, 3 * HD:MC], Bc[:, k, :], Bc[:, k, :], start=(k == 0),
                              stop=(k == KD - 1))
            i.then_inc(M_ps, 1)

            def transpose_low(count):
                pe.wait_ge(lstack_made, count)
                for n in range(NT):
                    i = pe.transpose(bankb(4 + n // 8)[0:KX, n % 8 * P:(n % 8 + 1) * P], lstack[:, n, :],
                                     identb[:, :])
                    if n % 8 == 7:
                        i.then_inc(lstackT_ps, 1)
                pe.wait_ge(lowTs_made, 2 * count)

            pe.wait_ge(ones_set, 3)
            transpose_low(1)
            pe.wait_ge(Ms_in, 16 * (TERMS + 3))
            for n in range(NT):
                i = pe.matmul(bank(0)[:, n * R:(n + 1) * R], lowTs0[0:KS, n * P:(n + 1) * P],
                              Ms[0:KS, 3 * HD:MC], start=True, stop=True)
            i.then_inc(y_ps, 1)
            transpose_low(2)
            def qkv_slot(s, r, i):
                if tile_live(r, 0):
                    if r >= 2:
                        pe.wait_ge(res1_made, s - 1)
                    pe.matmul(bank(r % 2)[:, 0:3 * HD], lowTs[0:KX, bass.ds(s * P, P)] if not isinstance(s, int) else
                              lowTs[0:KX, s * P:(s + 1) * P], Ms[0:KX, 0:3 * HD], start=True, stop=True)\
                        .then_inc(qkv_ps, 1)
                if tile_live(r, 2):
                    pe.wait_ge(stacks_made, s - 1)
                    if r >= 4:
                        pe.wait_ge(qT_made, s - 3)
                        pe.wait_ge(kT_made, s - 3)
                    for j, (st, rows) in enumerate(((qstack, KS), (kstack, KX))):
                        for h in range(H):
                            x = pe.transpose(bankb(4 + 2 * (r % 2) + j)[0:rows, h * P:(h + 1) * P],
                                             st[:, r % 2, h, 0:rows], identb[:, :])
                    x.then_inc(stackT_ps, 1)

            tiles(pe, qkv_slot, 4, 3)
            pe.wait_ge(qT_made, NT)
            pe.wait_ge(kT_made, NT)
            pe.wait_ge(v_made, NT)

            def head_slot(s, r, i):
                def scores(t):
                    if live(r, 0):
                        if r or t >= 2:
                            pe.wait_ge(max_made, s * TB + t - 1)
                        pe.matmul(bank(t % 2), qT[0:KS, s, t * P:(t + 1) * P], kT[0:KS, s, :],
                                  start=True, stop=True).then_inc(score_ps, 1)

                def scores_t(j):
                    if live(r, 2):
                        if j == 0:
                            pe.wait_ge(maxrow_made, s - 1)
                        if r >= 3:
                            pe.wait_ge(exhi_made, s * 2 - 5 + j)
                        for k in range(2):
                            x = pe.matmul(bank(2 + 2 * j + k), kT[0:KX, s - 2, (2 * j + k) * P:(2 * j + k + 1) * P],
                                          qT[0:KX, s - 2, :], start=True, stop=True)
                        x.then_inc(scoreT_ps, 1)

                scores_t(0)
                scores(0)
                scores(1)
                if live(r, 1):
                    pe.wait_ge(nparts_made, s * 3)
                    for t in range(TB):
                        x = pe.matmul(bank(6)[KS:KX, t * P:(t + 1) * P], nparts[:, (r - 1) % 2, :, t],
                                      identb[:, :], start=True, stop=True)
                    x.then_inc(maxrow_ps, 1)
                scores_t(1)
                scores(2)
                scores(3)
                if live(r, 3):
                    pe.wait_ge(exlo_dve, s - 2)
                    pe.wait_ge(exlo_pool, s - 2)
                    if r >= 4:
                        pe.wait_ge(o_made, s - 3)
                    for t in range(TB):
                        for k in range(TB):
                            for part_, ex in enumerate((exhi, exlo)):
                                x = pe.matmul(bank(7)[:, t * VC:(t + 1) * VC],
                                              ex[:, (r - 3) % 2, k, t * P:(t + 1) * P], vheads[:, k, s - 3, :],
                                              start=(k == 0 and part_ == 0), stop=(k == TB - 1 and part_ == 1))
                    x.then_inc(pv_ps, 1)

            heads(pe, head_slot)

            def norm_slot(s, r, i):
                if tile_live(r, 1):
                    p = (r - 1) % 2
                    pe.wait_ge(oT_made, s)
                    if r >= 3:
                        pe.wait_ge(h_made, s - 2)
                    ns = bass.ds((i * TB + (r - 1)) * P, P)
                    for j in range(2):
                        pe.matmul(bank(2 + 2 * p + j), lowTs0[0:KX, ns], Bs[0:KX, j * 512:(j + 1) * 512],
                                  start=True, stop=False)
                        x = pe.matmul(bank(2 + 2 * p + j), oT[:, p, :], woT[:, j * 512:(j + 1) * 512],
                                      start=False, stop=True)
                    x.then_inc(wo_ps, 1)
                if tile_live(r, 0):
                    pe.wait_ge(ocur_made, s + 1)
                    pe.transpose(bank(r % 2)[:, 0:HD], o_cur[:, r % 2, :], identf[:, :]).then_inc(oT_ps, 1)
                if tile_live(r, 3):
                    p = (r - 3) % 2
                    pe.wait_ge(xs_made, s - 2)
                    for j in range(2):
                        if r >= 4:
                            pe.wait_ge(xlo_made, s * 2 - 7 + j)
                        for k in range(4):
                            x = pe.transpose(bank(6 + j)[:, k * P:(k + 1) * P],
                                             xs[:, p, (4 * j + k) * P:(4 * j + k + 1) * P], identf[:, :])
                        x.then_inc(xsT_ps, 1)

            pe.wait_ge(wo_in, 16)
            pe.wait_ge(exhi_made, NU * 2)
            pe.wait_ge(Bs_in, 16 * (TERMS + 3))
            tiles(pe, norm_slot, 5, 4)
            pe.wait_ge(xlo_made, NT * 2)

            def slot(s, r, B):
                it, c, par = r % BI, r // BI % NB, r // PER_BLK % 2
                downs = []
                if LAG <= r < SLOTS + LAG:
                    dr = r - LAG
                    zpar, dpar, t0 = dr // BI % 2, dr // PER_BLK % 2, dr % BI * 2
                    downs = [(t, k, zp, wp, j) for t in range(2) for k in range(BI)
                             for zp, wp in ((0, 0), (0, 1), (1, 0)) for j in range(2)]
                half = len(downs) // 2

                def down(x):
                    t, k, zp, wp, j = downs[x]
                    if x == 0 and dr % PER_BLK == 0:
                        pe.wait_ge(wlo_made, B * DN_UNITS + DN_UNITS)
                    if x == 0 and dr % BI == 0:
                        pe.wait_ge(zlo_made, s - 1)
                    if x % half == 0:
                        pe.wait_ge(down_added, (s - LAG) * 2 + t + 1)
                    i = pe.matmul(bank(4 + 2 * t + j), zT[:, zpar, k, zp, (t0 + t) * P:(t0 + t + 1) * P],
                                  wdn[:, dpar, k, wp, j * 512:(j + 1) * 512],
                                  start=(k == 0 and (zp, wp) == (0, 0)),
                                  stop=(k == BI - 1 and (zp, wp) == (1, 0)))
                    if x % half == half - 1:
                        i.then_inc(down_ps, 1)

                for p, (o, _, m, k) in enumerate(GROUPS):
                    n = len(GROUPS)
                    for x in range(len(downs) * max(p - 2, 0) // (n - 2), len(downs) * max(p - 1, 0) // (n - 2)):
                        down(x)
                    if not has_groups(r):
                        continue
                    if p == 0 and r % PER_BLK < BI:
                        pe.wait_ge(gu_cast, B * GU_UNITS + (it + 1) * 4)
                    if p >= RING:
                        evac_wait(pe, s, p - RING)
                    elif r >= 1:
                        evac_wait(pe, s - 1, n + p - RING)
                    w = wgu[:, par, it, m, k * P:(k + 1) * P]
                    pe.matmul(bank(p % RING), w, xT[:, c, k, 0, :], start=True, stop=False)
                    pe.matmul(bank(p % RING), w, xT[:, c, k, 1, :], start=False, stop=True)\
                        .then_inc(group_ps, 1)

            schedule(pe, slot)


def kernel(x, L0_tok_A, L0_tok_B, L0_attn_Wqk_w, L0_attn_Wqk_b, L0_attn_Wv_w, L0_attn_Wv_b, L0_attn_Wo_w,
           L0_attn_Wo_b, L0_ffn_gate_q, L0_ffn_gate_s, L0_ffn_up_q, L0_ffn_up_s, L0_ffn_down_q, L0_ffn_down_s):
    import numpy as np
    import concourse.bacc as bacc
    from concourse.bass_utils import run_bass_kernel_spmd

    def arr(a):
        return np.asarray(a)

    nb, seq = x.shape
    D = L0_tok_B.shape[0]
    HD = L0_attn_Wv_w.shape[0]
    wqk = arr(L0_attn_Wqk_w).reshape(HD, 2, D)
    bqk = arr(L0_attn_Wqk_b).reshape(HD, 2)
    wqkv = np.concatenate([wqk[:, 0], wqk[:, 1], arr(L0_attn_Wv_w)], 0).T
    bqkv = np.concatenate([bqk[:, 0], bqk[:, 1], arr(L0_attn_Wv_b)])[None, :]

    def up_tiles(w):
        i, d = w.shape
        return arr(w).reshape(i // P, P, d // P, P).transpose(0, 3, 2, 1).reshape(i // P, P, d)

    def up_scales(s):
        i, g = s.shape
        return arr(s).reshape(i // (2 * P), 2, P, g).transpose(0, 2, 1, 3)

    gu_s = np.stack([up_scales(L0_ffn_gate_s), up_scales(L0_ffn_up_s)], 3)
    arrays = {
        "ids": arr(x).reshape(-1, P).T,
        "A_T": arr(L0_tok_A).T,
        "B_T": arr(L0_tok_B).T,
        "wqkv_T": wqkv,
        "qkv_b": bqkv,
        "wo_T": arr(L0_attn_Wo_w).T,
        "wo_b": arr(L0_attn_Wo_b),
        "gu_q": np.stack([up_tiles(L0_ffn_gate_q), up_tiles(L0_ffn_up_q)], 1),
        "gu_s": gu_s.reshape(gu_s.shape[0], P, -1),
        "dn_q": arr(L0_ffn_down_q).T.reshape(-1, P, D),
        "dn_s": arr(L0_ffn_down_s).T,
    }
    arrays = {k: np.ascontiguousarray(v) for k, v in arrays.items()}
    nc = bacc.Bacc("TRN2", target_bir_lowering=False, num_devices=1)
    args = [nc.dram_tensor(k, v.shape, mybir.dt.from_np(v.dtype), kind="ExternalInput").ap()
            for k, v in arrays.items()]
    out = nc.dram_tensor("out", (nb * seq, D), F32, kind="ExternalOutput").ap()
    lm_tower_kernel(nc, *args, out)
    got = run_bass_kernel_spmd(nc, [arrays], core_ids=[0])
    return got.results[0]["out"].reshape(nb, seq, D)
```
